# Optimizing a Trainium2 kernel written in Bass

```python
import numpy as np
import jax
import jax.numpy as jnp

def _softmax(x, axis=-1):
    return jax.nn.softmax(x, axis=axis)

def _gelu(x):
    return jax.nn.gelu(x, approximate=True)

def _silu(x):
    return jax.nn.silu(x)

def _sigmoid(x):
    return jax.nn.sigmoid(x)

def _layernorm(x, axis=-1, eps=1e-05):
    m = jnp.mean(x, axis=axis, keepdims=True)
    v = jnp.var(x, axis=axis, keepdims=True)
    return (x - m) / jnp.sqrt(v + eps)

def _scatter_add(tgt, idx, src, axis=0):
    return tgt.at[idx].add(src)

def _segment_sum(src, seg, n):
    return jax.ops.segment_sum(src, seg, n)
kernel_name = 'mk_gnn_preln_d2_gnn_r64_9d7b83'

def setup_inputs(seed: int=0):
    np.random.seed(seed)
    _w = jnp.asarray

    def _rec_inputs():
        import jax
        import jax.numpy as jnp
        _gk = jax.random.key(seed)
        x = -0.0001006 + 1 * jax.random.normal(jax.random.fold_in(_gk, 1), (100000, 96), jnp.float32)
        src = jax.random.randint(jax.random.fold_in(_gk, 2), (50000,), 0, 100000, jnp.int32)
        dst = jax.random.randint(jax.random.fold_in(_gk, 3), (50000,), 0, 100000, jnp.int32)
        _o = jnp.argsort(dst, stable=True)
        src = src[_o]
        dst = dst[_o]
        return (x, src, dst)
    x, src, dst = _rec_inputs()

    def _L0_gnn_setup():
        import jax, jax.numpy as jnp
        import numpy as np
        BN_EPS = 1e-05
        key = jax.random.key(seed)
        ks = jax.random.split(key, 5)
        N, E, D = (50000, 12500, 96)
        x = jax.random.normal(ks[0], (N, D), dtype=jnp.float32)
        edge_index = jax.random.randint(ks[1], (2, E), 0, N, dtype=jnp.int64)
        Wl = jax.random.normal(ks[2], (D, D), dtype=jnp.float32) / np.sqrt(D)
        bl = jnp.zeros((D,), dtype=jnp.float32)
        Wr = jax.random.normal(ks[3], (D, D), dtype=jnp.float32) / np.sqrt(D)
        gamma = jnp.ones((D,), dtype=jnp.float32)
        beta = jnp.zeros((D,), dtype=jnp.float32)
        return {'x': x, 'edge_index': edge_index, 'Wl': Wl, 'bl': bl, 'Wr': Wr, 'gamma': gamma, 'beta': beta}
    _L0_gnn_all = _L0_gnn_setup()
    _L0_gnn_in = {k: v for k, v in _L0_gnn_all.items() if k in ('Wl', 'bl', 'Wr', 'gamma', 'beta')}
    del _L0_gnn_all

    def _L1_gnn_setup():
        import jax, jax.numpy as jnp
        import numpy as np
        N_NODES = 50000
        N_EDGES = 12500
        D_IN = 96
        D_OUT = 96
        key = jax.random.key(seed)
        k1, k2, k3, k4 = jax.random.split(key, 4)
        x = jax.random.normal(k1, (N_NODES, D_IN), dtype=jnp.float32)
        edge_index = jax.random.randint(k2, (2, N_EDGES), 0, N_NODES, dtype=jnp.int64)
        W = jax.random.normal(k3, (D_IN, D_OUT), dtype=jnp.float32) * (1.0 / np.sqrt(D_IN))
        b = jax.random.normal(k4, (D_OUT,), dtype=jnp.float32) * 0.01
        return {'x': x, 'edge_index': edge_index, 'W': W, 'b': b}
    _L1_gnn_all = _L1_gnn_setup()
    _L1_gnn_in = {k: v for k, v in _L1_gnn_all.items() if k in ('W', 'b')}
    del _L1_gnn_all
    return {'x': x, 'src': src, 'dst': dst, 'L0_gnn_Wl': _L0_gnn_in['Wl'], 'L0_gnn_bl': _L0_gnn_in['bl'], 'L0_gnn_Wr': _L0_gnn_in['Wr'], 'L0_gnn_gamma': _L0_gnn_in['gamma'], 'L0_gnn_beta': _L0_gnn_in['beta'], 'L1_gnn_W': _L1_gnn_in['W'], 'L1_gnn_b': _L1_gnn_in['b']}

def reference(x, src, dst, L0_gnn_Wl, L0_gnn_bl, L0_gnn_Wr, L0_gnn_gamma, L0_gnn_beta, L1_gnn_W, L1_gnn_b):
    import jax
    import jax.numpy as jnp

    def _L0_gnn_ref(x, edge_index, Wl, bl, Wr, gamma, beta):
        import jax, jax.numpy as jnp
        import numpy as np
        BN_EPS = 1e-05
        N = x.shape[0]
        src, dst = (edge_index[0], edge_index[1])
        msg_sum = jax.ops.segment_sum(x[src], dst, num_segments=N)
        deg = jax.ops.segment_sum(jnp.ones_like(src, dtype=x.dtype), dst, num_segments=N)
        neigh_mean = msg_sum / jnp.maximum(deg, 1.0)[:, None]
        h = jnp.einsum('nd,od->no', neigh_mean, Wl) + bl + jnp.einsum('nd,od->no', x, Wr)
        mu = h.mean(axis=0)
        var = h.var(axis=0)
        h = (h - mu) * jax.lax.rsqrt(var + BN_EPS) * gamma + beta
        return jax.nn.relu(h)

    def _L1_gnn_ref(x, edge_index, W, b):
        import jax, jax.numpy as jnp
        import numpy as np
        N_NODES = 50000
        N_EDGES = 12500
        D_IN = 96
        D_OUT = 96
        num_nodes = x.shape[0]
        src, dst = (edge_index[0], edge_index[1])
        messages = x[src] @ W + b
        out = jax.ops.segment_sum(messages, dst, num_segments=num_nodes)
        deg = jax.ops.segment_sum(jnp.ones((dst.shape[0],), dtype=x.dtype), dst, num_segments=num_nodes)
        deg = jnp.clip(deg, 1.0, None)
        return out / deg[:, None]
    edge_index = jnp.stack([src, dst])
    h = jnp.maximum(_layernorm(x, axis=-1), 0.0)
    x = x + _L0_gnn_ref(h, edge_index, L0_gnn_Wl, L0_gnn_bl, L0_gnn_Wr, L0_gnn_gamma, L0_gnn_beta)
    h = jnp.maximum(_layernorm(x, axis=-1), 0.0)
    x = x + _L1_gnn_ref(h, edge_index, L1_gnn_W, L1_gnn_b)
    return x

_drawn_inputs = setup_inputs


def setup_inputs(seed=0):
    import zlib

    import numpy as np

    out = dict(_drawn_inputs(seed))
    spreads = {'L0_gnn_bl': (0.0, 0.8), 'L0_gnn_gamma': (1.0, 0.2), 'L0_gnn_beta': (0.0, 0.1)}
    factors = {'L1_gnn_b': 8.0}
    for name, (base, spread) in spreads.items():
        noise = np.random.default_rng([zlib.crc32(name.encode()), seed]).standard_normal(out[name].shape)
        drawn = base * np.exp(spread * noise) if base else spread * noise
        out[name] = jnp.asarray(drawn.astype(out[name].dtype))
    for name, factor in factors.items():
        out[name] = (out[name] * factor).astype(out[name].dtype)
    return out
```

```python
import numpy as np

import concourse.bass as bass
from concourse import mybir
from contextlib import ExitStack, contextmanager

F32 = mybir.dt.float32
I32 = mybir.dt.int32
U32 = mybir.dt.uint32
ALU = mybir.AluOpType
ACT = mybir.ActivationFunctionType
AX = mybir.AxisListType

P = 128
D = 96
N = 100000
E = 50000
BLOCK = 2 * P
BLOCKS = 4
SUB = 2 * BLOCKS
NODES = BLOCK * BLOCKS
STEPS = -(-N // NODES)
CH = 4
EDGES = CH * P
assert STEPS * EDGES >= E
NPAD = STEPS * NODES
EPAD = STEPS * EDGES
TILES = CH + SUB
MSG = D + 2
WINDOW = BLOCK
GROUP = 16
GROUPS = EDGES // GROUP
EPS = 1e-5
FAR = float(1 << 20)
UNROLL = 6
LAG = 5
SUMS_ROW = EPAD + WINDOW
TABLE = SUMS_ROW + NPAD
TAIL = N - (STEPS - 1) * NODES
TAIL_BLOCKS = TAIL // BLOCK
TAIL_PARTS = (TAIL - TAIL_BLOCKS * BLOCK) // 2


class Step:

    def __init__(self, j, k):
        if isinstance(j, int):
            j, k = 0, UNROLL * j + k
        else:
            while k < 0:
                j, k = j - 1, k + UNROLL
            while k >= UNROLL:
                j, k = j + 1, k - UNROLL
        self.j, self.k = j, k
        self.fixed = isinstance(j, int)
        self.n = k if self.fixed else j * UNROLL + k
        self.half = k // 2 if self.fixed else j * (UNROLL // 2) + k // 2
        self.par = k % 2
        self.ring = k % UNROLL

    def back(self, d):
        return Step(self.j, self.k - d)

    def exists(self, steps=STEPS):
        return not self.fixed or 0 <= self.k < steps


def wait(eng, sem, value):
    if not isinstance(value, int) or value > 0:
        eng.wait_ge(sem, value)


def run_steps(eng, body):
    first = UNROLL + 2
    loops = (STEPS - 2 - first) // UNROLL
    for s in range(first):
        body(Step(0, s))
    with eng.Fori(1, 1 + loops) as j:
        for k in range(2, UNROLL + 2):
            body(Step(j, k))
    for s in range(first + UNROLL * loops, STEPS + LAG + 2):
        body(Step(0, s))


@contextmanager
def stage(nc, tag=""):
    sems = []

    def sem(name):
        sems.append(nc.alloc_semaphore(name + tag))
        return sems[-1]

    with ExitStack() as st:
        yield st, sem
        nc.clear_and_free_semaphores(sems)
        nc.all_engine_barrier()


def settle(eng, passed):
    eng.sem_inc(passed, 1)


def rows(ap, start, count, per):
    return ap[bass.ds(start, count * per), :].rearrange("(p j) d -> p (j d)", j=per)


def gnn_kernel(nc, x, src, dst, wl_t, bl, wr_t, gamma, beta, w, b, out):
    h_dram = nc.dram_tensor("h_dram", [NPAD, D], F32).ap()
    xsrc_dram = nc.dram_tensor("xsrc_dram", [EPAD, D], F32).ap()
    msg_dram = [nc.dram_tensor(f"msg{i}_dram", [TABLE, MSG], F32).ap() for i in range(2)]
    group_dram = nc.dram_tensor("group_dram", [2, STEPS * GROUPS], F32).ap()
    start_dram = nc.dram_tensor("start_dram", [1, STEPS * BLOCKS], I32).ap()

    ctx = ExitStack()
    with ctx:
        def sb(name, shape, dt=F32, stack=ctx):
            return stack.enter_context(nc.sbuf_tensor(name, shape, dt))

        ident = sb("ident", [P, P])
        ones = sb("ones", [P, P])
        iota = sb("iota", [P, 2, P])
        negbase = sb("negbase", [P, STEPS * BLOCKS])
        eps = sb("eps", [P, 1])
        weights = sb("weights", [D, 3, D])
        vectors = sb("vectors", [P, 4, D])
        src_col = sb("src_col", [P, STEPS, CH], U32)
        dst_col = sb("dst_col", [P, STEPS, CH])
        starts_all = sb("starts_all", [1, STEPS * BLOCKS], I32)
        starts_none = sb("starts_none", [1, STEPS * BLOCKS], I32)
        unfit = sb("unfit", [1, 1], I32)
        node_col = sb("node_col", [P, 2])
        inv_deg = sb("inv_deg", [P, STEPS, SUB])
        bn = sb("bn", [P, 2, D])
        sums = sb("sums", [P, 2, SUB * D])

        with stage(nc) as (st, sem):
            def tb(name, shape, dt=F32):
                return sb(name, shape, dt, st)

            idx_int = tb("idx_int", [STEPS, 2, EDGES], I32)
            idx_f = tb("idx_f", [STEPS, 2, EDGES])
            next_int = tb("next_int", [STEPS, EDGES], I32)
            next_f = tb("next_f", [STEPS, EDGES])
            iota_int = tb("iota_int", [P, 2, P], I32)
            base_int = tb("base_int", [P, STEPS * BLOCKS], I32)
            row_base = tb("row_base", [P, 4])
            row_base_int = tb("row_base_int", [P, 4], I32)
            extremes = tb("extremes", [STEPS, 2, GROUPS])
            all_ext = tb("all_ext", [P, 2, STEPS * GROUPS])
            cmp_out = tb("cmp_out", [P, STEPS * GROUPS])
            below = tb("below", [P, 4])
            start_f = tb("start_f", [P, 4])
            start_i = tb("start_i", [P, 4], I32)
            pad = tb("pad", [P, 2, MSG])
            above = tb("above", [P, 4])
            base_end = tb("base_end", [P, 4])
            sums_start = tb("sums_start", [P, 4])
            node_int = tb("node_int", [P, 2], I32)
            limit_int = tb("limit_int", [P, 1], I32)
            limit = tb("limit", [P, 1])
            bad = tb("bad", [P, 3, 4])
            bad_total = tb("bad_total", [P, 1])
            fits = tb("fits", [P, 1])
            disorder = tb("disorder", [STEPS, EDGES])
            ps = st.enter_context(nc.psum_tensor("ps_idx", [P, 8, 512], F32))
            loaded = sem("setup_loaded")
            ext_saved = sem("ext_saved")
            ext_loaded = sem("ext_loaded")
            start_saved = sem("start_saved")
            start_loaded = sem("start_loaded")
            pads_saved = sem("pads_saved")
            cleared = sem("setup_cleared")
            consts = sem("setup_consts")
            dve = sem("setup_dve")
            turned = sem("setup_turned")
            judged = sem("judged")
            START_DONE = 33
            full = E // EDGES
            rest = E - full * EDGES

            with nc.Block() as block:
                @block.sync
                def _(sp):
                    for i, v in enumerate((wl_t, wr_t, w)):
                        sp.dma_start(weights[:, i, :], v).then_inc(loaded, 16)
                    for i, v in enumerate((bl, gamma, beta, b)):
                        sp.dma_start(vectors[:, i, :], v.rearrange("(a d) -> a d", a=1).to_broadcast([P, D])).then_inc(loaded, 16)
                    sp.wait_ge(cleared, 1)
                    for i, v in enumerate((src, dst)):
                        sp.dma_start(idx_int[0:full, i, :], v[0:full * EDGES].rearrange("(s e) -> s e", e=EDGES)).then_inc(loaded, 16)
                        sp.dma_start(idx_int[full:full + 1, i, 0:rest], v[full * EDGES:E].rearrange("(s e) -> s e", s=1)).then_inc(loaded, 16)
                    sp.wait_ge(cleared, 2)
                    sp.dma_start(next_int[0:full, :], dst[1:1 + full * EDGES].rearrange("(s e) -> s e", e=EDGES)).then_inc(loaded, 16)
                    sp.dma_start(next_int[full:full + 1, 0:rest - 1], dst[full * EDGES + 1:E].rearrange("(s e) -> s e", s=1)).then_inc(loaded, 16)
                    sp.wait_ge(dve, 3)
                    sp.dma_start(group_dram.rearrange("i (s g) -> s i g", g=GROUPS), extremes[:, :, :]).then_inc(ext_saved, 16)
                    sp.wait_ge(ext_saved, 16)
                    for i in range(2):
                        sp.dma_start(all_ext[:, i, :], group_dram[i:i + 1, :].to_broadcast([P, STEPS * GROUPS])).then_inc(ext_loaded, 16)
                    sp.wait_ge(dve, START_DONE)
                    sp.dma_start(start_dram.rearrange("i (s b) -> (i s) b", b=BLOCKS), start_i[0:STEPS, :]).then_inc(start_saved, 16)
                    sp.wait_ge(start_saved, 16)
                    sp.dma_start(starts_all[:, :], start_dram).then_inc(start_loaded, 16)
                    sp.wait_ge(start_loaded, 16)
                    sp.wait_ge(consts, 6)
                    for m in msg_dram:
                        sp.dma_start(rows(m, EPAD, P, 2), pad[:, :, :].rearrange("p j d -> p (j d)")).then_inc(pads_saved, 16)
                    sp.wait_ge(pads_saved, 32)
                    sp.wait_ge(loaded, 16 * 13)

                @block.gpsimd
                def _(pool):
                    pool.memset(idx_int[:, 0, :], 0).then_inc(consts, 1)
                    pool.memset(idx_int[:, 1, :], int(FAR)).then_inc(cleared, 1)
                    pool.memset(next_int[:, :], int(FAR)).then_inc(cleared, 1)
                    pool.iota(iota_int[:, :, :], pattern=[[1, 2], [2, P]], base=0, channel_multiplier=0).then_inc(consts, 1)
                    pool.iota(base_int[:, :], pattern=[[-BLOCK, STEPS * BLOCKS]], base=0, channel_multiplier=0).then_inc(consts, 1)
                    pool.iota(row_base_int[:, :], pattern=[[BLOCK, 4]], base=0, channel_multiplier=NODES).then_inc(consts, 1)
                    pool.memset(pad[:, :, :], FAR).then_inc(consts, 1)
                    pool.memset(ident[:, :], 0.0).then_inc(consts, 1)
                    pool.wait_ge(consts, 6)
                    pool.affine_select(out=ident[:, :], in_=ident[:, :], compare_op=ALU.not_equal, fill=1.0, base=0,
                                       pattern=[[-1, P]], channel_multiplier=1).then_inc(consts, 1)
                    pool.memset(ones[:, :], 1.0).then_inc(consts, 1)
                    pool.memset(eps[:, :], EPS).then_inc(consts, 1)
                    pool.memset(starts_none[:, :], EPAD).then_inc(consts, 1)
                    pool.iota(node_int[:, :], pattern=[[1, 2]], base=0, channel_multiplier=2).then_inc(consts, 1)
                    pool.iota(limit_int[:, :], pattern=[[1, 1]], base=(LAG - 2) * EDGES, channel_multiplier=EDGES).then_inc(consts, 1)

                @block.vector
                def _(v):
                    done = [0]

                    def then(ins):
                        done[0] += 1
                        ins.then_inc(dve, 1)
                        v.wait_ge(dve, done[0])

                    v.wait_ge(loaded, 16 * 13)
                    then(v.tensor_copy(idx_f[:, :, :], idx_int[:, :, :]))
                    grouped = idx_f[:, 1, :].rearrange("s (g e) -> s g e", e=GROUP)
                    then(v.tensor_reduce(extremes[:, 0, :], grouped, axis=AX.X, op=ALU.min))
                    then(v.tensor_reduce(extremes[:, 1, :], grouped, axis=AX.X, op=ALU.max))
                    v.wait_ge(consts, 12)
                    then(v.tensor_copy(iota[:, :, :], iota_int[:, :, :]))
                    then(v.tensor_copy(negbase[:, :], base_int[:, :]))
                    then(v.tensor_copy(row_base[:, :], row_base_int[:, :]))
                    then(v.tensor_copy(node_col[:, :], node_int[:, :]))
                    then(v.tensor_copy(limit[:, :], limit_int[:, :]))
                    then(v.tensor_scalar(base_end[:, :], row_base[:, :], float(BLOCK), None, ALU.add))
                    then(v.tensor_scalar(sums_start[:, :], row_base[:, :], float(SUMS_ROW), None, ALU.add))
                    v.wait_ge(ext_loaded, 32)
                    for g in range(BLOCKS):
                        then(v.tensor_scalar(cmp_out[:, :], all_ext[:, 1, :], row_base[:, g:g + 1], None, ALU.is_lt,
                                             ALU.add, accum_out=below[:, g:g + 1]))
                        then(v.tensor_scalar(cmp_out[:, :], all_ext[:, 0, :], base_end[:, g:g + 1], None, ALU.is_lt,
                                             ALU.add, accum_out=above[:, g:g + 1]))
                    then(v.tensor_scalar(start_f[:, :], below[:, :], float(GROUP), None, ALU.mult))
                    then(v.memset(bad[:, :, :], 0.0))
                    then(v.tensor_tensor(above[:, :], above[:, :], below[:, :], ALU.subtract))
                    then(v.tensor_scalar(bad[0:STEPS, 0, :], above[0:STEPS, :], float(WINDOW // GROUP), None, ALU.is_gt))
                    then(v.tensor_scalar(above[:, :], start_f[:, :], float(WINDOW), float(EPAD), ALU.add, ALU.min))
                    then(v.tensor_scalar(bad[0:STEPS, 1, :], above[0:STEPS, :], limit[0:STEPS, :], None, ALU.is_gt))
                    then(v.tensor_copy(next_f[:, :], next_int[:, :]))
                    then(v.tensor_tensor(disorder[:, :], idx_f[:, 1, :], next_f[:, :], ALU.is_gt))
                    then(v.tensor_reduce(bad[0:STEPS, 2, 0:1], disorder[:, :], axis=AX.X, op=ALU.max))
                    then(v.tensor_reduce(bad_total[:, :], bad[:, :, :], axis=AX.XY, op=ALU.add))
                    v.wait_ge(judged, 1)
                    then(v.tensor_scalar(fits[:, :], ps[:, 0, 0:1], 0.5, None, ALU.is_lt))
                    then(v.tensor_scalar(unfit[:, :], ps[0:1, 0, 0:1], 0.5, None, ALU.is_gt))
                    then(v.tensor_tensor(start_f[:, :], start_f[:, :], sums_start[:, :], ALU.subtract))
                    then(v.scalar_tensor_tensor(out=start_f[:, :], in0=start_f[:, :], scalar=fits[:, :], in1=sums_start[:, :],
                                                op0=ALU.mult, op1=ALU.add))
                    then(v.tensor_copy(start_i[:, :], start_f[:, :]))
                    assert done[0] == START_DONE
                    v.wait_ge(turned, 8)
                    for c in range(CH):
                        then(v.tensor_copy(src_col[:, :, c], ps[:, c, 0:STEPS]))
                        then(v.tensor_copy(dst_col[:, :, c], ps[:, CH + c, 0:STEPS]))

                @block.tensor
                def _(pe):
                    pe.wait_ge(consts, 8)
                    pe.wait_ge(dve, START_DONE - 5)
                    pe.matmul(ps[:, 0, 0:1], ones[:, :], bad_total[:, :], start=True, stop=True).then_inc(judged, 1)
                    pe.wait_ge(dve, START_DONE)
                    for i in range(2):
                        for c in range(CH):
                            pe.transpose(ps[:, CH * i + c, 0:STEPS], idx_f[:, i, :].rearrange("s (p c) -> s c p", c=CH)[:, c, :],
                                         ident[0:STEPS, 0:STEPS]).then_inc(turned, 1)

        PER_LOAD = 7
        LOADS = STEPS // PER_LOAD
        assert LOADS * PER_LOAD == STEPS

        def sum_all_pairs(table, tag):
            with stage(nc, tag) as (st, sem):
                edges = sb("pairs_edges" + tag, [P, PER_LOAD, CH * MSG], F32, st)
                sel = sb("pairs_sel" + tag, [P, CH, BLOCKS, 2, P], F32, st)
                node_rows = sb("pairs_rows" + tag, [P, BLOCKS, 2, MSG], F32, st)
                zeros = sb("pairs_zeros" + tag, [P, 512], F32, st)
                ps = st.enter_context(nc.psum_tensor("pairs_ps" + tag, [P, BLOCKS, 512], F32))
                loaded, stored, rows_ready, sel_ready, used, summed, zeroed, sp_passed, dve_passed = (
                    sem("pairs_" + n) for n in
                    ("loaded", "stored", "rows_ready", "sel_ready", "used", "summed", "zeroed", "sp_passed", "dve_passed"))

                with nc.Block() as block:
                    @block.sync
                    def _(sp):
                        with sp.Fori(0, STEPS) as t:
                            with sp.Fori(0, LOADS) as g:
                                sp.wait_ge(used, t * (STEPS + 1) + g * PER_LOAD + 1)
                                sp.dma_start(edges[:, :, :], table[bass.ds(g * (PER_LOAD * EDGES), PER_LOAD * EDGES), :]
                                             .rearrange("(e p c) m -> p e (c m)", p=P, c=CH)).then_inc(loaded, 16)
                            sp.wait_ge(rows_ready, t + 1)
                            sp.dma_start(table[bass.ds(t * NODES + SUMS_ROW, NODES), :].rearrange("(b p j) m -> p b (j m)", p=P, j=2),
                                         node_rows[:, :, :, :].rearrange("p b j m -> p b (j m)")).then_inc(stored, 16)
                            sp.wait_ge(stored, 16 * t + 16)
                            settle(sp, sp_passed)

                    @block.gpsimd
                    def _(pool):
                        pool.memset(zeros[:, :], 0.0).then_inc(zeroed, 1)

                    @block.vector
                    def _(v):
                        with v.Fori(0, STEPS) as t:
                            with v.Fori(0, LOADS) as g:
                                v.wait_ge(loaded, t * (16 * LOADS) + g * 16 + 16)
                                settle(v, dve_passed)
                                with v.Fori(0, PER_LOAD) as e:
                                    v.wait_ge(used, t * (STEPS + 1) + g * PER_LOAD + e + 1)
                                    for c in range(CH):
                                        for b in range(BLOCKS):
                                            last = v.tensor_scalar(
                                                sel[:, c, b, :, :], iota[:, :, :],
                                                edges[:, bass.ds(e, 1), c * MSG + D + 1:c * MSG + D + 2].rearrange("p e m -> p (e m)"),
                                                negbase[:, bass.ds(t * BLOCKS + b, 1)], ALU.subtract, ALU.is_equal)
                                    last.then_inc(sel_ready, 1)
                            v.wait_ge(used, t * (STEPS + 1) + STEPS + 1)
                            v.tensor_copy(node_rows[:, :, :, 0:D + 1], ps[:, :, 0:2 * P].rearrange("p b (j d) -> p b j d", j=2)[:, :, :, 0:D + 1]
                                          ).then_inc(summed, 1)
                            for b in range(BLOCKS):
                                last = v.tensor_scalar(node_rows[:, b, :, D + 1], node_col[:, :], negbase[:, bass.ds(t * BLOCKS + b, 1)], None,
                                                       ALU.subtract)
                            last.then_inc(rows_ready, 1)

                    @block.tensor
                    def _(pe):
                        pe.wait_ge(zeroed, 1)
                        pe.sem_inc(summed, 1)
                        with pe.Fori(0, STEPS) as t:
                            pe.wait_ge(summed, t + 1)
                            for b in range(BLOCKS):
                                last = pe.matmul(ps[:, b, :], zeros[:, 0:P], zeros[:, :], start=True, stop=False, skip_group_check=True)
                            last.then_inc(used, 1)
                            with pe.Fori(0, STEPS) as e:
                                pe.wait_ge(sel_ready, t * STEPS + e + 1)
                                for c in range(CH):
                                    for b in range(BLOCKS):
                                        for j in range(2):
                                            last = pe.matmul(ps[:, b, j * P:j * P + D + 1], sel[:, c, b, j, :],
                                                             edges[:, bass.ds(e % PER_LOAD, 1), c * MSG:c * MSG + D + 1].rearrange("p e m -> p (e m)"),
                                                             start=False, stop=False, skip_group_check=True)
                                last.then_inc(used, 1)

        def layer0(starts, tag):
            with stage(nc, tag) as (st, sem):
                def tb(name, shape, dt=F32):
                    return sb(name + tag, shape, dt, st)

                def pb(name, banks):
                    return st.enter_context(nc.psum_tensor(name + tag, [P, banks, 512], F32))

                idx = [tb(f"idx{i}", [P, CH], U32) for i in range(2)]
                gathered = [tb(f"gathered{i}", [P, CH, D]) for i in range(2)]
                own = [tb(f"own{i}", [P, SUB, D]) for i in range(2)]
                ln_raw = tb("ln_raw", [P, TILES, 6])
                ln_tmp = tb("ln_tmp", [P, 4, TILES])
                mean2 = tb("mean2", [P, TILES])
                std = [tb(f"std{i}", [P, TILES]) for i in range(2)]
                rstd = [tb(f"rstd{i}", [P, TILES]) for i in range(2)]
                centred = [tb(f"centred{i}", [P, TILES, D]) for i in range(2)]
                turned_x = [tb(f"turned_x{i}", [D, TILES * P]) for i in range(2)]
                msg = [tb(f"msg{i}", [P, CH, MSG]) for i in range(2)]
                h = [tb(f"h{i}", [P, SUB, D]) for i in range(UNROLL)]
                agg = tb("agg", [P, SUB, D])
                deg = tb("deg", [P, SUB])
                inv = tb("inv", [P, SUB])
                h_sq = tb("h_sq", [P, SUB, D])
                win = [tb(f"win{i}", [P, BLOCKS, 2, MSG]) for i in range(2)]
                sel = tb("sel", [P, BLOCKS, 2, 2, P])
                ps_t = pb("ps_t", 3)
                ps_m = pb("ps_m", 3)
                ps_a = pb("ps_a", 2)

                sp_passed = sem("sp_passed")
                pool_passed = sem("pool_passed")
                idx_ready = sem("idx_ready")
                g_loaded = [sem(f"g_loaded{i}") for i in range(2)]
                own_loaded = [sem(f"own_loaded{i}") for i in range(2)]
                own_cleared = sem("own_cleared")
                xs_stored = [sem(f"xs_stored{i}") for i in range(2)]
                ln_sem = sem("ln_sem")
                std_ready = sem("std_ready")
                rstd_ready = sem("rstd_ready")
                centred_ready = sem("centred_ready")
                t_ready = sem("t_ready")
                tx_ready = sem("tx_ready")
                m_ready = sem("m_ready")
                msg_ready = sem("msg_ready")
                msg_init = sem("msg_init")
                msg_stored = [sem(f"msg_stored{i}") for i in range(2)]
                hd_ready = sem("hd_ready")
                win_loaded = [sem(f"win_loaded{i}") for i in range(2)]
                sel_ready = sem("sel_ready")
                agg_ready = sem("agg_ready")
                inv_sem = sem("inv_sem")
                agg_scaled = sem("agg_scaled")
                h_ready = sem("h_ready")
                sq_ready = sem("sq_ready")
                summed = sem("summed")
                h_stored = [sem(f"h_stored{i}") for i in range(2)]

                def block_rows(ap, n, b):
                    return rows(ap, n * NODES + b * BLOCK, P, 2)

                with nc.Block() as block:
                    @block.sync
                    def _(sp):
                        def load_own(s):
                            wait(sp, centred_ready, 2 * s.back(2).n + 2)
                            if s.fixed and s.k == STEPS - 1:
                                wait(sp, own_cleared, 1)
                                for b in range(TAIL_BLOCKS):
                                    sp.dma_start(own[s.par][:, 2 * b:2 * b + 2, :].rearrange("p j d -> p (j d)"),
                                                 block_rows(x, s.n, b)).then_inc(own_loaded[s.par], 16)
                                sp.dma_start(own[s.par][0:TAIL_PARTS, 2 * TAIL_BLOCKS:2 * TAIL_BLOCKS + 2, :].rearrange("p j d -> p (j d)"),
                                             rows(x, s.n * NODES + TAIL_BLOCKS * BLOCK, TAIL_PARTS, 2)).then_inc(own_loaded[s.par], 16)
                            else:
                                sp.dma_start(own[s.par][:, :, :].rearrange("p (b j) d -> p b (j d)", j=2),
                                             x[bass.ds(s.n * NODES, NODES), :].rearrange("(b p j) d -> p b (j d)", p=P, j=2)
                                             ).then_inc(own_loaded[s.par], 16)

                        def load_windows(t):
                            m = t.back(-2)
                            used = 2 * t.n - 2
                            if not t.fixed:
                                used = sp.snap(used)
                            if t.fixed and t.k == 0:
                                for k in range(2):
                                    sp.wait_ge(msg_stored[k], 16)
                            if m.exists():
                                wait(sp, msg_stored[m.par], 16 * (m.half + 1))
                            if not t.fixed:
                                settle(sp, sp_passed)
                            wait(sp, agg_ready, used)
                            if not t.fixed:
                                settle(sp, sp_passed)
                            for b in range(BLOCKS):
                                start = sp.value_load(starts[0:1, bass.ds(t.n * BLOCKS + b, 1)], min_val=0, max_val=TABLE - WINDOW)
                                sp.dma_start(win[t.par][:, b, :, :].rearrange("p j d -> p (j d)"),
                                             rows(msg_dram[0], start, P, 2)).then_inc(win_loaded[t.par], 16)

                        def step(s):
                            if s.fixed and s.k == 0:
                                load_own(s)
                            if s.back(4).exists():
                                load_windows(s.back(4))
                            if s.back(-1).exists():
                                load_own(s.back(-1))
                            if s.exists():
                                wait(sp, g_loaded[s.par], 16 * CH * (s.half + 1))
                                sp.dma_start(rows(xsrc_dram, s.n * EDGES, P, CH),
                                             gathered[s.par][:, :, :].rearrange("p c d -> p (c d)")).then_inc(xs_stored[s.par], 16)
                            m = s.back(1)
                            if m.exists():
                                wait(sp, msg_ready, 2 * m.n + 2)
                                if m.fixed and m.k < 2:
                                    sp.wait_ge(msg_init, 2)
                                sp.dma_start(rows(msg_dram[0], m.n * EDGES, P, CH),
                                             msg[m.par][:, :, :].rearrange("p c d -> p (c d)")).then_inc(msg_stored[m.par], 16)
                            t = s.back(LAG + 1)
                            if t.exists():
                                wait(sp, h_ready, t.n + 1)
                                sp.dma_start(h_dram[bass.ds(t.n * NODES, NODES), :].rearrange("(b p j) d -> p b (j d)", p=P, j=2),
                                             h[t.ring][:, :, :].rearrange("p (b j) d -> p b (j d)", j=2)).then_inc(h_stored[t.par], 16)

                        run_steps(sp, step)
                        for k in range(2):
                            sp.wait_ge(h_stored[k], 16 * (STEPS // 2))
                            sp.wait_ge(xs_stored[k], 16 * (STEPS // 2))
                            sp.wait_ge(msg_stored[k], 16 * (STEPS // 2))

                    @block.gpsimd
                    def _(pool):
                        def gather(s):
                            wait(pool, idx_ready, s.n + 1)
                            wait(pool, centred_ready, 2 * s.back(2).n + 1)
                            wait(pool, xs_stored[s.par], 16 * s.half)
                            settle(pool, pool_passed)
                            for c in range(CH):
                                pool.indirect_dma_start(
                                    out=gathered[s.par][:, c, :], out_offset=None, in_=x,
                                    in_offset=bass.IndirectOffsetOnAxis(ap=idx[s.par][:, c:c + 1], axis=0)).then_inc(g_loaded[s.par], 16)

                        def step(s):
                            if s.fixed and s.k == 0:
                                gather(s)
                            if s.back(-1).exists():
                                gather(s.back(-1))
                            t = s.back(LAG + 1)
                            if t.exists():
                                wait(pool, h_ready, t.n + 1)
                                wait(pool, summed, 2 * t.n)
                                pool.tensor_tensor(sums[:, 0, :], sums[:, 0, :], h[t.ring][:, :, :].rearrange("p a d -> p (a d)"),
                                                   ALU.add).then_inc(summed, 1)
                                wait(pool, sq_ready, t.n + 1)
                                pool.tensor_tensor(sums[:, 1, :], sums[:, 1, :], h_sq[:, :, :].rearrange("p a d -> p (a d)"),
                                                   ALU.add).then_inc(summed, 1)

                        for i in range(2):
                            pool.memset(msg[i][:, :, D:D + 1], 1.0).then_inc(msg_init, 1)
                        pool.memset(sums[:, :, :], 0.0).then_inc(msg_init, 1)
                        pool.wait_ge(msg_init, 3)
                        run_steps(pool, step)

                    @block.vector
                    def _(v):
                        def copy_idx(s):
                            v.tensor_copy(idx[s.par][:, :], src_col[:, bass.ds(s.n, 1), :].rearrange("p s c -> p (s c)")).then_inc(idx_ready, 1)

                        def step(s):
                            t = s.back(LAG + 1)
                            if t.exists():
                                wait(v, agg_ready, 2 * t.n + 2)
                                v.tensor_scalar(deg[:, :], ps_a[:, :, :].rearrange("p k (a d) -> p k a d", a=4)[:, :, :, D].rearrange("p k a -> p k a"),
                                                1.0, None, ALU.max).then_inc(inv_sem, 1)
                                wait(v, inv_sem, 3 * t.n + 1)
                                wait(v, agg_scaled, 2 * t.n)
                                v.reciprocal(inv[:, :], deg[:, :]).then_inc(inv_sem, 1)
                                wait(v, inv_sem, 3 * t.n + 2)
                                v.tensor_scalar(inv_deg[:, bass.ds(t.n, 1), :].rearrange("p s a -> p (s a)"), inv[:, :],
                                                1.0, None, ALU.mult).then_inc(inv_sem, 1)
                            if s.fixed and s.k == 0:
                                copy_idx(s)
                                copy_idx(s.back(-1))
                            if s.exists():
                                wait(v, g_loaded[s.par], 16 * CH * (s.half + 1))
                                if s.back(-2).exists():
                                    copy_idx(s.back(-2))
                                for c in range(CH):
                                    v.bn_stats(ln_raw[:, c, :], gathered[s.par][:, c, :])
                                wait(v, own_loaded[s.par], 16 * (s.half + 1 + (TAIL_BLOCKS if s.fixed and s.k == STEPS - 1 else 0)))
                                for c in range(SUB):
                                    last = v.bn_stats(ln_raw[:, CH + c, :], own[s.par][:, c, :])
                                last.then_inc(ln_sem, 1)
                                wait(v, ln_sem, 4 * s.n + 1)
                                even, odd = ln_raw[:, :, 1], ln_raw[:, :, 4]
                                v.tensor_tensor(mean2[:, :], even, odd, ALU.add)
                                v.tensor_tensor(ln_tmp[:, 0, :], even, odd, ALU.subtract)
                                v.tensor_tensor(ln_tmp[:, 1, :], ln_raw[:, :, 2], ln_raw[:, :, 5], ALU.add).then_inc(ln_sem, 1)
                                wait(v, ln_sem, 4 * s.n + 2)
                                v.tensor_tensor(ln_tmp[:, 2, :], ln_tmp[:, 0, :], ln_tmp[:, 0, :], ALU.mult).then_inc(ln_sem, 1)
                                wait(v, ln_sem, 4 * s.n + 3)
                                wait(v, std_ready, s.n)
                                v.scalar_tensor_tensor(out=ln_tmp[:, 3, :], in0=ln_tmp[:, 2, :], scalar=D / 4.0, in1=ln_tmp[:, 1, :],
                                                       op0=ALU.mult, op1=ALU.add).then_inc(ln_sem, 1)
                            m = s.back(1)
                            if m.exists():
                                wait(v, m_ready, 3 * m.n + 1)
                                wait(v, msg_stored[m.par], 16 * m.half)
                                v.tensor_tensor(msg[m.par][:, :, 0:D], ps_m[:, 0, 0:CH * D].rearrange("p (c d) -> p c d", d=D),
                                                rstd[m.par][:, 0:CH].unsqueeze(2).to_broadcast([P, CH, D]), ALU.mult).then_inc(msg_ready, 1)
                                v.tensor_copy(msg[m.par][:, :, D + 1], dst_col[:, bass.ds(m.n, 1), :].rearrange("p s c -> p (s c)")).then_inc(msg_ready, 1)
                            if s.exists():
                                wait(v, std_ready, s.n + 1)
                                v.reciprocal(rstd[s.par][:, :], std[s.par][:, :]).then_inc(rstd_ready, 1)
                                wait(v, t_ready, 3 * s.back(2).n + 3)
                                v.scalar_tensor_tensor(out=centred[s.par][:, 0:CH, :], in0=mean2[:, 0:CH].unsqueeze(2).to_broadcast([P, CH, D]),
                                                       scalar=-0.5, in1=gathered[s.par][:, :, :], op0=ALU.mult, op1=ALU.add).then_inc(centred_ready, 1)
                                v.scalar_tensor_tensor(out=centred[s.par][:, CH:TILES, :], in0=mean2[:, CH:TILES].unsqueeze(2).to_broadcast([P, SUB, D]),
                                                       scalar=-0.5, in1=own[s.par][:, :, :], op0=ALU.mult, op1=ALU.add).then_inc(centred_ready, 1)
                                if s.fixed and s.k == STEPS - 3:
                                    v.wait_ge(centred_ready, 2 * (STEPS - 2))
                                    v.memset(own[s.par][:, :, :], 0.0).then_inc(own_cleared, 1)
                            if t.exists():
                                wait(v, agg_scaled, 2 * t.n + 2)
                                wait(v, hd_ready, 2 * t.n + 2)
                                v.tensor_tensor(h[t.ring][:, :, :], h[t.ring][:, :, :], agg[:, :, :], ALU.add).then_inc(h_ready, 1)
                            u = s.back(LAG)
                            if u.exists():
                                wait(v, win_loaded[u.par], 16 * BLOCKS * (u.half + 1))
                                wait(v, agg_ready, 2 * u.n)
                                for b in range(BLOCKS):
                                    for i in range(2):
                                        last = v.tensor_scalar(sel[:, b, i, :, :], iota[:, :, :], win[u.par][:, b, i, D + 1:D + 2],
                                                               negbase[:, bass.ds(u.n * BLOCKS + b, 1)], ALU.subtract, ALU.is_equal)
                                    last.then_inc(sel_ready, 1)

                        run_steps(v, step)

                    @block.scalar
                    def _(act):
                        def step(s):
                            m, t = s.back(1), s.back(LAG + 1)
                            if s.exists():
                                wait(act, ln_sem, 4 * s.n + 4)
                                act.activation(std[s.par][:, :], ln_tmp[:, 3, :], ACT.Sqrt, scale=1.0 / D, bias=eps[:, :]).then_inc(std_ready, 1)
                            if m.exists():
                                r = m.back(UNROLL)
                                wait(act, h_stored[r.par], 16 * (r.half + 1))
                                wait(act, summed, 2 * r.n + 2)
                                wait(act, rstd_ready, m.n + 1)
                                for k in range(2):
                                    wait(act, m_ready, 3 * m.n + 2 + k)
                                    for c in range(4):
                                        a = 4 * k + c
                                        last = act.activation(h[m.ring][:, a, :], ps_m[:, 1 + k, c * D:(c + 1) * D], ACT.Copy,
                                                              scale=rstd[m.par][:, CH + a:CH + a + 1])
                                    last.then_inc(hd_ready, 1)
                            if t.exists():
                                wait(act, inv_sem, 3 * t.n + 2)
                                wait(act, h_ready, t.n)
                                for k in range(2):
                                    for c in range(4):
                                        a = 4 * k + c
                                        last = act.activation(agg[:, a, :], ps_a[:, k, c * P:c * P + D], ACT.Copy,
                                                              scale=inv[:, a:a + 1])
                                    last.then_inc(agg_scaled, 1)
                            if s.exists():
                                for k in range(3):
                                    wait(act, t_ready, 3 * s.n + 1 + k)
                                    if k == 0:
                                        wait(act, m_ready, 3 * s.back(2).n + 3)
                                    act.activation(turned_x[s.par][:, k * 512:(k + 1) * 512], ps_t[0:D, k, :], ACT.Relu).then_inc(tx_ready, 1)
                            if t.exists():
                                wait(act, h_ready, t.n + 1)
                                wait(act, summed, 2 * t.n)
                                act.activation(h_sq[:, :, :], h[t.ring][:, :, :], ACT.Square).then_inc(sq_ready, 1)

                        run_steps(act, step)

                    @block.tensor
                    def _(pe):
                        def step(s):
                            m = s.back(1)
                            if m.exists():
                                for k in range(3):
                                    wait(pe, tx_ready, 3 * m.n + 1 + k)
                                    if k == 0:
                                        wait(pe, msg_ready, 2 * m.n)
                                    else:
                                        wait(pe, hd_ready, 2 * m.back(1).n + k)
                                    for c in range(4):
                                        a = 4 * k + c
                                        last = pe.matmul(ps_m[:, k, c * D:(c + 1) * D], turned_x[m.par][:, a * P:(a + 1) * P],
                                                         weights[:, 0 if k == 0 else 1, :], start=True, stop=True)
                                    last.then_inc(m_ready, 1)
                            if s.exists():
                                for k in range(3):
                                    wait(pe, centred_ready, 2 * s.n + (1 if k == 0 else 2))
                                    wait(pe, tx_ready, 3 * s.back(1).n + 1 + k)
                                    for c in range(4):
                                        last = pe.transpose(ps_t[0:D, k, c * P:(c + 1) * P], centred[s.par][:, 4 * k + c, :], ident[:, :])
                                    last.then_inc(t_ready, 1)
                            u = s.back(LAG)
                            if u.exists():
                                wait(pe, win_loaded[u.par], 16 * BLOCKS * (u.half + 1))
                                for k in range(2):
                                    wait(pe, agg_scaled, 2 * u.back(1).n + 1 + k)
                                    for b in (2 * k, 2 * k + 1):
                                        wait(pe, sel_ready, 4 * u.n + b + 1)
                                        for j in range(2):
                                            c = 2 * (b % 2) + j
                                            for i in range(2):
                                                last = pe.matmul(ps_a[:, k, c * P:c * P + D + 1], sel[:, b, i, j, :],
                                                                 win[u.par][:, b, i, 0:D + 1], start=(i == 0), stop=(i == 1))
                                    last.then_inc(agg_ready, 1)

                        run_steps(pe, step)

        def batch_norm():
            with stage(nc) as (st, sem):
                part = sb("bn_part", [P, 2, D], F32, st)
                moment = sb("bn_moment", [P, 2, D], F32, st)
                tmp = sb("bn_tmp", [P, 4, D], F32, st)
                ps = st.enter_context(nc.psum_tensor("ps_bn", [P, 512], F32))
                dve, total, root = sem("bn_dve"), sem("bn_total"), sem("bn_root")
                with nc.Block() as block:
                    @block.vector
                    def _(v):
                        done = [0]

                        def then(ins):
                            done[0] += 1
                            ins.then_inc(dve, 1)
                            v.wait_ge(dve, done[0])

                        then(v.tensor_reduce(part[:, :, :], sums[:, :, :].rearrange("p i (a d) -> p i d a", d=D), axis=AX.X, op=ALU.add))
                        v.wait_ge(total, 1)
                        then(v.tensor_scalar(moment[:, :, :], ps[:, 0:2 * D].rearrange("p (i d) -> p i d", d=D), 1.0 / N, None, ALU.mult))
                        then(v.tensor_tensor(tmp[:, 0, :], moment[:, 0, :], moment[:, 0, :], ALU.mult))
                        then(v.tensor_tensor(tmp[:, 1, :], moment[:, 1, :], tmp[:, 0, :], ALU.subtract))
                        then(v.tensor_scalar(tmp[:, 1, :], tmp[:, 1, :], 0.0, None, ALU.max))
                        v.wait_ge(root, 1)
                        then(v.reciprocal(tmp[:, 2, :], tmp[:, 2, :]))
                        then(v.tensor_tensor(bn[:, 0, :], tmp[:, 2, :], vectors[:, 1, :], ALU.mult))
                        then(v.tensor_tensor(moment[:, 0, :], moment[:, 0, :], vectors[:, 0, :], ALU.add))
                        then(v.tensor_tensor(tmp[:, 3, :], vectors[:, 0, :], moment[:, 0, :], ALU.subtract))
                        then(v.tensor_tensor(tmp[:, 3, :], tmp[:, 3, :], bn[:, 0, :], ALU.mult))
                        then(v.tensor_tensor(bn[:, 1, :], tmp[:, 3, :], vectors[:, 2, :], ALU.add))

                    @block.tensor
                    def _(pe):
                        pe.wait_ge(dve, 1)
                        pe.matmul(ps[:, 0:2 * D], ones[:, :], part[:, :, :].rearrange("p i d -> p (i d)"), start=True, stop=True).then_inc(total, 1)

                    @block.scalar
                    def _(act):
                        act.wait_ge(dve, 5)
                        act.activation(tmp[:, 2, :], tmp[:, 1, :], ACT.Sqrt, bias=eps[:, :]).then_inc(root, 1)

        def layer1(starts, tag):
            with stage(nc, tag) as (st, sem):
                def tb(name, shape, dt=F32):
                    return sb(name + tag, shape, dt, st)

                def pb(name, banks):
                    return st.enter_context(nc.psum_tensor(name + tag, [P, banks, 512], F32))

                idx = [tb(f"idx1_{i}", [P, CH], U32) for i in range(2)]
                gathered = [tb(f"h_src{i}", [P, CH, D]) for i in range(2)]
                xs = [tb(f"x_src{i}", [P, CH, D]) for i in range(2)]
                x2 = [tb(f"x2_src{i}", [P, CH, D]) for i in range(2)]
                ln_raw = tb("ln1_raw", [P, CH, 6])
                ln_tmp = tb("ln1_tmp", [P, 4, CH])
                mean2 = tb("mean2_1", [P, CH])
                std = [tb(f"std1_{i}", [P, CH]) for i in range(2)]
                rstd = [tb(f"rstd1_{i}", [P, CH]) for i in range(2)]
                centred = [tb(f"centred1_{i}", [P, CH, D]) for i in range(2)]
                turned_x = [tb(f"turned1_{i}", [D, CH * P]) for i in range(2)]
                msg = [tb(f"msg1_{i}", [P, CH, MSG]) for i in range(2)]
                xn = [tb(f"x_own{i}", [P, SUB, D]) for i in range(3)]
                hn = [tb(f"h_own{i}", [P, SUB, D]) for i in range(3)]
                agg = tb("agg1", [P, SUB, D])
                win = [tb(f"win1_{i}", [P, BLOCKS, 2, MSG]) for i in range(2)]
                sel = tb("sel1", [P, BLOCKS, 2, 2, P])
                ps_t = pb("ps1_t", 2)
                ps_m = pb("ps1_m", 2)
                ps_a = pb("ps1_a", 4)

                sp_passed = sem("sp1_passed")
                pool_passed = sem("pool1_passed")
                idx_ready = sem("idx1_ready")
                g_loaded = [sem(f"h_src_loaded{i}") for i in range(2)]
                xs_loaded = [sem(f"x_src_loaded{i}") for i in range(2)]
                x2_ready = sem("x2_ready")
                ln_sem = sem("ln1_sem")
                std_ready = sem("std1_ready")
                rstd_ready = sem("rstd1_ready")
                centred_ready = sem("centred1_ready")
                t_ready = sem("t1_ready")
                tx_ready = sem("tx1_ready")
                m_ready = sem("m1_ready")
                scaled = sem("msg1_scaled")
                msg_ready = sem("msg1_ready")
                msg_stored = [sem(f"msg1_stored{i}") for i in range(2)]
                msg_init = sem("msg1_init")
                own_cleared = sem("own1_cleared")
                xn_loaded = [sem(f"x_own_loaded{i}") for i in range(3)]
                hn_loaded = [sem(f"h_own_loaded{i}") for i in range(3)]
                win_loaded = [sem(f"win1_loaded{i}") for i in range(2)]
                normed = sem("normed")
                sel_ready = sem("sel1_ready")
                agg_ready = sem("agg1_ready")
                agg_scaled = sem("agg1_scaled")
                out_ready = sem("out_ready")
                out_stored = [sem(f"out_stored{i}") for i in range(3)]

                def third(t):
                    return t.ring % 3, (t.k // 3 if t.fixed else t.j * (UNROLL // 3) + t.k // 3)

                with nc.Block() as block:
                    @block.sync
                    def _(sp):
                        def load_xs(s):
                            wait(sp, x2_ready, 3 * s.back(2).n + 3)
                            sp.dma_start(xs[s.par][:, :, :].rearrange("p c d -> p (c d)"), rows(xsrc_dram, s.n * EDGES, P, CH)
                                         ).then_inc(xs_loaded[s.par], 16)

                        def load_nodes(t):
                            slot, uses = third(t)
                            wait(sp, out_stored[slot], 16 * uses)
                            if t.fixed and t.k == STEPS - 1:
                                sp.wait_ge(own_cleared, 1)
                                for b in range(TAIL_BLOCKS):
                                    sp.dma_start(xn[slot][:, 2 * b:2 * b + 2, :].rearrange("p j d -> p (j d)"),
                                                 rows(x, t.n * NODES + b * BLOCK, P, 2)).then_inc(xn_loaded[slot], 16)
                                sp.dma_start(xn[slot][0:TAIL_PARTS, 2 * TAIL_BLOCKS:2 * TAIL_BLOCKS + 2, :].rearrange("p j d -> p (j d)"),
                                             rows(x, t.n * NODES + TAIL_BLOCKS * BLOCK, TAIL_PARTS, 2)).then_inc(xn_loaded[slot], 16)
                            else:
                                sp.dma_start(xn[slot][:, :, :].rearrange("p (b j) d -> p b (j d)", j=2),
                                             x[bass.ds(t.n * NODES, NODES), :].rearrange("(b p j) d -> p b (j d)", p=P, j=2)
                                             ).then_inc(xn_loaded[slot], 16)
                            sp.dma_start(hn[slot][:, :, :].rearrange("p (b j) d -> p b (j d)", j=2),
                                         h_dram[bass.ds(t.n * NODES, NODES), :].rearrange("(b p j) d -> p b (j d)", p=P, j=2)
                                         ).then_inc(hn_loaded[slot], 16)

                        def load_windows(t):
                            m = t.back(-2)
                            used = 4 * t.n - 4
                            if not t.fixed:
                                used = sp.snap(used)
                            if t.fixed and t.k == 0:
                                for k in range(2):
                                    sp.wait_ge(msg_stored[k], 16)
                            if m.exists():
                                wait(sp, msg_stored[m.par], 16 * (m.half + 1))
                            if not t.fixed:
                                settle(sp, sp_passed)
                            wait(sp, agg_ready, used)
                            if not t.fixed:
                                settle(sp, sp_passed)
                            for b in range(BLOCKS):
                                start = sp.value_load(starts[0:1, bass.ds(t.n * BLOCKS + b, 1)], min_val=0, max_val=TABLE - WINDOW)
                                sp.dma_start(win[t.par][:, b, :, :].rearrange("p j d -> p (j d)"),
                                             rows(msg_dram[1], start, P, 2)).then_inc(win_loaded[t.par], 16)

                        def step(s):
                            if s.fixed and s.k == 0:
                                load_xs(s)
                            if s.back(4).exists():
                                load_windows(s.back(4))
                            if s.back(-1).exists():
                                load_xs(s.back(-1))
                            if s.back(4).exists():
                                load_nodes(s.back(4))
                            m = s.back(1)
                            if m.exists():
                                wait(sp, msg_ready, 2 * m.n + 2)
                                if m.fixed and m.k < 2:
                                    sp.wait_ge(msg_init, 2)
                                sp.dma_start(rows(msg_dram[1], m.n * EDGES, P, CH),
                                             msg[m.par][:, :, :].rearrange("p c d -> p (c d)")).then_inc(msg_stored[m.par], 16)
                            t = s.back(LAG + 1)
                            if t.exists():
                                slot, _ = third(t)
                                wait(sp, out_ready, 2 * t.n + 2)
                                if t.fixed and t.k == STEPS - 1:
                                    for b in range(TAIL_BLOCKS):
                                        sp.dma_start(rows(out, t.n * NODES + b * BLOCK, P, 2),
                                                     xn[slot][:, 2 * b:2 * b + 2, :].rearrange("p j d -> p (j d)")).then_inc(out_stored[slot], 16)
                                    sp.dma_start(rows(out, t.n * NODES + TAIL_BLOCKS * BLOCK, TAIL_PARTS, 2),
                                                 xn[slot][0:TAIL_PARTS, 2 * TAIL_BLOCKS:2 * TAIL_BLOCKS + 2, :].rearrange("p j d -> p (j d)")
                                                 ).then_inc(out_stored[slot], 16)
                                else:
                                    sp.dma_start(out[bass.ds(t.n * NODES, NODES), :].rearrange("(b p j) d -> p b (j d)", p=P, j=2),
                                                 xn[slot][:, :, :].rearrange("p (b j) d -> p b (j d)", j=2)).then_inc(out_stored[slot], 16)

                        run_steps(sp, step)
                        for k in range(2):
                            sp.wait_ge(msg_stored[k], 16 * (STEPS // 2))
                        for slot in range(3):
                            uses = len(range(slot, STEPS, 3)) + (TAIL_BLOCKS if slot == (STEPS - 1) % 3 else 0)
                            sp.wait_ge(out_stored[slot], 16 * uses)

                    @block.gpsimd
                    def _(pool):
                        def gather(s):
                            wait(pool, idx_ready, s.n + 1)
                            wait(pool, x2_ready, 3 * s.back(2).n + 3)
                            settle(pool, pool_passed)
                            for c in range(CH):
                                pool.indirect_dma_start(
                                    out=gathered[s.par][:, c, :], out_offset=None, in_=h_dram,
                                    in_offset=bass.IndirectOffsetOnAxis(ap=idx[s.par][:, c:c + 1], axis=0)).then_inc(g_loaded[s.par], 16)

                        def step(s):
                            if s.fixed and s.k == 0:
                                gather(s)
                            if s.back(-1).exists():
                                gather(s.back(-1))
                            u = s.back(LAG)
                            if u.exists():
                                slot, uses = third(u)
                                wait(pool, hn_loaded[slot], 16 * (uses + 1))
                                pool.tensor_tensor(hn[slot][:, :, :], hn[slot][:, :, :], bn[:, 0, :].unsqueeze(1).to_broadcast([P, SUB, D]),
                                                   ALU.mult).then_inc(normed, 1)
                                wait(pool, normed, 2 * u.n + 1)
                                pool.tensor_tensor(hn[slot][:, :, :], hn[slot][:, :, :], bn[:, 1, :].unsqueeze(1).to_broadcast([P, SUB, D]),
                                                   ALU.add).then_inc(normed, 1)

                        for i in range(2):
                            pool.memset(msg[i][:, :, D:D + 1], 1.0).then_inc(msg_init, 1)
                        run_steps(pool, step)

                    @block.vector
                    def _(v):
                        def copy_idx(s):
                            v.tensor_copy(idx[s.par][:, :], src_col[:, bass.ds(s.n, 1), :].rearrange("p s c -> p (s c)")).then_inc(idx_ready, 1)

                        def step(s):
                            t = s.back(LAG + 1)
                            if s.fixed and s.k == 0:
                                copy_idx(s)
                                copy_idx(s.back(-1))
                            if s.exists():
                                wait(v, g_loaded[s.par], 16 * CH * (s.half + 1))
                                if s.back(-2).exists():
                                    copy_idx(s.back(-2))
                                g, z = gathered[s.par], x2[s.par]
                                wait(v, centred_ready, s.n - 1)
                                v.tensor_tensor(z[:, :, :], g[:, :, :], bn[:, 0, :].unsqueeze(1).to_broadcast([P, CH, D]), ALU.mult).then_inc(x2_ready, 1)
                                wait(v, x2_ready, 3 * s.n + 1)
                                v.tensor_tensor(z[:, :, :], z[:, :, :], bn[:, 1, :].unsqueeze(1).to_broadcast([P, CH, D]), ALU.add).then_inc(x2_ready, 1)
                                wait(v, x2_ready, 3 * s.n + 2)
                                wait(v, xs_loaded[s.par], 16 * (s.half + 1))
                                v.scalar_tensor_tensor(out=z[:, :, :], in0=z[:, :, :], scalar=0.0, in1=xs[s.par][:, :, :],
                                                       op0=ALU.max, op1=ALU.add).then_inc(x2_ready, 1)
                                wait(v, x2_ready, 3 * s.n + 3)
                                for c in range(CH):
                                    last = v.bn_stats(ln_raw[:, c, :], z[:, c, :])
                                last.then_inc(ln_sem, 1)
                                wait(v, ln_sem, 4 * s.n + 1)
                                even, odd = ln_raw[:, :, 1], ln_raw[:, :, 4]
                                v.tensor_tensor(mean2[:, :], even, odd, ALU.add)
                                v.tensor_tensor(ln_tmp[:, 0, :], even, odd, ALU.subtract)
                                v.tensor_tensor(ln_tmp[:, 1, :], ln_raw[:, :, 2], ln_raw[:, :, 5], ALU.add).then_inc(ln_sem, 1)
                                wait(v, ln_sem, 4 * s.n + 2)
                                v.tensor_tensor(ln_tmp[:, 2, :], ln_tmp[:, 0, :], ln_tmp[:, 0, :], ALU.mult).then_inc(ln_sem, 1)
                                wait(v, ln_sem, 4 * s.n + 3)
                                wait(v, std_ready, s.n)
                                v.scalar_tensor_tensor(out=ln_tmp[:, 3, :], in0=ln_tmp[:, 2, :], scalar=D / 4.0, in1=ln_tmp[:, 1, :],
                                                       op0=ALU.mult, op1=ALU.add).then_inc(ln_sem, 1)
                            m = s.back(1)
                            if m.exists():
                                wait(v, scaled, m.n + 1)
                                v.tensor_tensor(msg[m.par][:, :, 0:D], msg[m.par][:, :, 0:D], vectors[:, 3, :].unsqueeze(1).to_broadcast([P, CH, D]),
                                                ALU.add).then_inc(msg_ready, 1)
                                v.tensor_copy(msg[m.par][:, :, D + 1], dst_col[:, bass.ds(m.n, 1), :].rearrange("p s c -> p (s c)")).then_inc(msg_ready, 1)
                            if s.exists():
                                wait(v, std_ready, s.n + 1)
                                v.reciprocal(rstd[s.par][:, :], std[s.par][:, :]).then_inc(rstd_ready, 1)
                                wait(v, t_ready, s.n - 1)
                                v.scalar_tensor_tensor(out=centred[s.par][:, :, :], in0=mean2[:, :].unsqueeze(2).to_broadcast([P, CH, D]),
                                                       scalar=-0.5, in1=x2[s.par][:, :, :], op0=ALU.mult, op1=ALU.add).then_inc(centred_ready, 1)
                            if t.exists():
                                slot, uses = third(t)
                                wait(v, normed, 2 * t.n + 2)
                                wait(v, xn_loaded[slot], 16 * (uses + 1 + (TAIL_BLOCKS if t.fixed and t.k == STEPS - 1 else 0)))
                                v.scalar_tensor_tensor(out=xn[slot][:, :, :], in0=hn[slot][:, :, :], scalar=0.0, in1=xn[slot][:, :, :],
                                                       op0=ALU.max, op1=ALU.add).then_inc(out_ready, 1)
                                wait(v, out_ready, 2 * t.n + 1)
                                wait(v, agg_scaled, 4 * t.n + 4)
                                v.tensor_tensor(xn[slot][:, :, :], xn[slot][:, :, :], agg[:, :, :], ALU.add).then_inc(out_ready, 1)
                                if t.fixed and t.k == STEPS - 4:
                                    for q in range(1):
                                        v.wait_ge(out_stored[slot], 16 * (uses + 1))
                                    v.memset(xn[slot][:, :, :], 0.0).then_inc(own_cleared, 1)
                            u = s.back(LAG)
                            if u.exists():
                                wait(v, win_loaded[u.par], 16 * BLOCKS * (u.half + 1))
                                wait(v, agg_ready, 4 * u.n)
                                for b in range(BLOCKS):
                                    for i in range(2):
                                        last = v.tensor_scalar(sel[:, b, i, :, :], iota[:, :, :], win[u.par][:, b, i, D + 1:D + 2],
                                                               negbase[:, bass.ds(u.n * BLOCKS + b, 1)], ALU.subtract, ALU.is_equal)
                                    last.then_inc(sel_ready, 1)

                        run_steps(v, step)

                    @block.scalar
                    def _(act):
                        def step(s):
                            m, t = s.back(1), s.back(LAG + 1)
                            if s.exists():
                                wait(act, ln_sem, 4 * s.n + 4)
                                act.activation(std[s.par][:, :], ln_tmp[:, 3, :], ACT.Sqrt, scale=1.0 / D, bias=eps[:, :]).then_inc(std_ready, 1)
                            if m.exists():
                                wait(act, m_ready, m.n + 1)
                                wait(act, rstd_ready, m.n + 1)
                                wait(act, msg_stored[m.par], 16 * m.half)
                                for c in range(CH):
                                    last = act.activation(msg[m.par][:, c, 0:D], ps_m[:, m.par, c * D:(c + 1) * D], ACT.Copy, scale=rstd[m.par][:, c:c + 1])
                                last.then_inc(scaled, 1)
                            if t.exists():
                                wait(act, out_ready, 2 * t.n)
                                for b in range(BLOCKS):
                                    wait(act, agg_ready, 4 * t.n + b + 1)
                                    for j in range(2):
                                        a = 2 * b + j
                                        last = act.activation(agg[:, a, :], ps_a[:, b, j * P:j * P + D], ACT.Copy,
                                                              scale=inv_deg[:, bass.ds(t.n, 1), a:a + 1].rearrange("p s a -> p (s a)"))
                                    last.then_inc(agg_scaled, 1)
                            if s.exists():
                                wait(act, t_ready, s.n + 1)
                                wait(act, m_ready, s.n - 1)
                                act.activation(turned_x[s.par][:, :], ps_t[0:D, s.par, :], ACT.Relu).then_inc(tx_ready, 1)

                        run_steps(act, step)

                    @block.tensor
                    def _(pe):
                        def step(s):
                            m = s.back(1)
                            if m.exists():
                                wait(pe, tx_ready, m.n + 1)
                                wait(pe, scaled, m.n - 1)
                                for c in range(CH):
                                    last = pe.matmul(ps_m[:, m.par, c * D:(c + 1) * D], turned_x[m.par][:, c * P:(c + 1) * P],
                                                     weights[:, 2, :], start=True, stop=True)
                                last.then_inc(m_ready, 1)
                            if s.exists():
                                wait(pe, centred_ready, s.n + 1)
                                wait(pe, tx_ready, s.n - 1)
                                for c in range(CH):
                                    last = pe.transpose(ps_t[0:D, s.par, c * P:(c + 1) * P], centred[s.par][:, c, :], ident[:, :])
                                last.then_inc(t_ready, 1)
                            u = s.back(LAG)
                            if u.exists():
                                wait(pe, win_loaded[u.par], 16 * BLOCKS * (u.half + 1))
                                for b in range(BLOCKS):
                                    wait(pe, agg_scaled, 4 * u.back(1).n + b + 1)
                                    wait(pe, sel_ready, 4 * u.n + b + 1)
                                    for j in range(2):
                                        for i in range(2):
                                            last = pe.matmul(ps_a[:, b, j * P:j * P + D + 1], sel[:, b, i, j, :],
                                                             win[u.par][:, b, i, 0:D + 1], start=(i == 0), stop=(i == 1))
                                    last.then_inc(agg_ready, 1)

                        run_steps(pe, step)

        misfit = nc.values_load(unfit[0:1, 0:1], min_val=0, max_val=1)
        with nc.If(misfit > 0):
            layer0(starts_none, "_a")
            sum_all_pairs(msg_dram[0], "_0")
        layer0(starts_all, "")
        batch_norm()
        with nc.If(misfit > 0):
            layer1(starts_none, "_a")
            sum_all_pairs(msg_dram[1], "_1")
        layer1(starts_all, "")


def kernel(x, src, dst, L0_gnn_Wl, L0_gnn_bl, L0_gnn_Wr, L0_gnn_gamma, L0_gnn_beta, L1_gnn_W, L1_gnn_b):
    import concourse.bacc as bacc
    from concourse.bass_utils import run_bass_kernel_spmd

    nc = bacc.Bacc("TRN2", target_bir_lowering=False, num_devices=1)
    given = {
        "x": x, "src": src, "dst": dst, "wl_t": np.transpose(L0_gnn_Wl), "bl": L0_gnn_bl,
        "wr_t": np.transpose(L0_gnn_Wr), "gamma": L0_gnn_gamma, "beta": L0_gnn_beta,
        "w": L1_gnn_W, "b": L1_gnn_b,
    }
    arrays, args = {}, []
    for name, a in given.items():
        a = np.ascontiguousarray(a)
        arrays[f"in_{name}"] = a
        args.append(nc.dram_tensor(f"in_{name}", a.shape, mybir.dt.from_np(a.dtype), kind="ExternalInput").ap())
    result = nc.dram_tensor("result", [N, D], F32, kind="ExternalOutput").ap()
    gnn_kernel(nc, *args, result)
    r = run_bass_kernel_spmd(nc, [arrays], core_ids=[0])
    return r.results[0]["result"]
```

```python
import numpy as np

import concourse.bass as bass
from concourse import mybir
from contextlib import ExitStack, contextmanager

F32 = mybir.dt.float32
I32 = mybir.dt.int32
U32 = mybir.dt.uint32
ALU = mybir.AluOpType
ACT = mybir.ActivationFunctionType
AX = mybir.AxisListType

P = 128
D = 96
N = 100000
E = 50000
BLOCK = 2 * P
BLOCKS = 4
SUB = 2 * BLOCKS
HALF = P
HALVES = BLOCK // HALF * BLOCKS
NODES = BLOCK * BLOCKS
STEPS = -(-N // NODES)
CH = 4
EDGES = CH * P
assert STEPS * EDGES >= E
NPAD = STEPS * NODES
EPAD = STEPS * EDGES
TILES = CH + SUB
MSG = 128
WINDOW = P
GROUP = 16
GROUPS = EDGES // GROUP
EPS = 1e-5
FAR = float(1 << 20)
POOL_SHIFTS = 6
UNROLL = 8
LAG = 6
AHEAD = 3
SUMS_ROW = EPAD + WINDOW
TABLE = SUMS_ROW + NPAD
TAIL = N - (STEPS - 1) * NODES
TAIL_BLOCKS = TAIL // BLOCK
TAIL_PARTS = (TAIL - TAIL_BLOCKS * BLOCK) // 2


class Step:

    def __init__(self, j, k):
        if isinstance(j, int):
            j, k = 0, UNROLL * j + k
        else:
            while k < 0:
                j, k = j - 1, k + UNROLL
            while k >= UNROLL:
                j, k = j + 1, k - UNROLL
        self.j, self.k = j, k
        self.fixed = isinstance(j, int)
        self.n = k if self.fixed else j * UNROLL + k
        self.half = k // 2 if self.fixed else j * (UNROLL // 2) + k // 2
        self.par = k % 2
        self.ring = k % UNROLL
        self.slot = k % 4
        self.uses = k // 4 if self.fixed else j * (UNROLL // 4) + k // 4

    def back(self, d):
        return Step(self.j, self.k - d)

    def exists(self, steps=STEPS):
        return not self.fixed or 0 <= self.k < steps


def wait(eng, sem, value):
    if not isinstance(value, int) or value > 0:
        eng.wait_ge(sem, value)


def run_steps(eng, body):
    loops = (STEPS - 1) // UNROLL
    for s in range(UNROLL):
        body(Step(0, s))
    with eng.Fori(1, loops) as j:
        for k in range(UNROLL):
            body(Step(j, k))
    for s in range(UNROLL * loops, STEPS + LAG + 2):
        body(Step(0, s))


@contextmanager
def stage(nc, tag=""):
    sems = []

    def sem(name):
        sems.append(nc.alloc_semaphore(name + tag))
        return sems[-1]

    with ExitStack() as st:
        yield st, sem
        nc.clear_and_free_semaphores(sems)
        nc.all_engine_barrier()


def settle(eng, passed):
    eng.sem_inc(passed, 1)


def rows(ap, start, count, per):
    return ap[bass.ds(start, count * per), :].rearrange("(p j) d -> p (j d)", j=per)


def load_step_windows(nc, sp, table, pairs, tile, loaded):
    _, pairs = nc.values_load_multi_w_load_instructions(pairs, engines=[mybir.EngineType.SP], min_val=0, max_val=TABLE - WINDOW)
    for b, pair in enumerate(pairs):
        apart = pair % GROUP
        for h, start in enumerate((pair - apart, pair + apart * (GROUP - 1))):
            start = sp.snap(start).with_bounds(min_val=0, max_val=TABLE - WINDOW)
            sp.dma_start(tile[:, 2 * b + h, :], rows(table, start, P, 1)).then_inc(loaded, 16)


def gnn_kernel(nc, x, src, dst, wl_t, bl, wr_t, gamma, beta, w, b, out):
    h_dram = nc.dram_tensor("h_dram", [NPAD, D + 1], F32).ap()
    xsrc_dram = nc.dram_tensor("xsrc_dram", [EPAD, D], F32).ap()
    msg_dram = [nc.dram_tensor(f"msg{i}_dram", [TABLE, MSG], F32).ap() for i in range(2)]
    group_dram = nc.dram_tensor("group_dram", [1, STEPS * GROUPS], F32).ap()
    start_dram = nc.dram_tensor("start_dram", [1, STEPS * BLOCKS], I32).ap()

    ctx = ExitStack()
    with ctx:
        def sb(name, shape, dt=F32, stack=ctx):
            return stack.enter_context(nc.sbuf_tensor(name, shape, dt))

        ident = sb("ident", [P, P])
        ones = sb("ones", [P, P])
        iota = sb("iota", [P, 2, P])
        negbase = sb("negbase", [P, STEPS * BLOCKS])
        negbase_half = sb("negbase_half", [P, STEPS * HALVES])
        eps = sb("eps", [P, 1])
        weights = sb("weights", [D, 3, D])
        vectors = sb("vectors", [D, 3, 1])
        b_row = sb("b_row", [P, D])
        src_col = sb("src_col", [P, STEPS, CH], U32)
        dst_col = sb("dst_col", [P, STEPS, CH])
        starts_all = sb("starts_all", [1, STEPS * BLOCKS], I32)
        starts_none = sb("starts_none", [1, STEPS * BLOCKS], I32)
        unfit = sb("unfit", [1, 1], I32)
        node_col = sb("node_col", [P, 2])
        inv_deg = sb("inv_deg", [P, STEPS, SUB])
        bn = sb("bn", [P, 2, D])
        gram = sb("gram", [D, D + 1])

        with stage(nc) as (st, sem):
            def tb(name, shape, dt=F32):
                return sb(name, shape, dt, st)

            idx_int = tb("idx_int", [STEPS, 2, EDGES], I32)
            idx_f = tb("idx_f", [STEPS, 2, EDGES])
            next_int = tb("next_int", [STEPS, EDGES], I32)
            next_f = tb("next_f", [STEPS, EDGES])
            iota_int = tb("iota_int", [P, 2, P], I32)
            base_int = tb("base_int", [P, STEPS * BLOCKS], I32)
            half_int = tb("half_int", [P, STEPS * HALVES], I32)
            row_base = tb("row_base", [P, HALVES + 1])
            row_base_int = tb("row_base_int", [P, HALVES + 1], I32)
            highest = tb("highest", [STEPS, GROUPS])
            all_highest = tb("all_highest", [P, STEPS * GROUPS])
            cmp_out = tb("cmp_out", [P, STEPS * GROUPS])
            below = tb("below", [P, HALVES + 1])
            start_f = tb("start_f", [P, HALVES])
            start_pair = tb("start_pair", [P, BLOCKS])
            start_i = tb("start_i", [P, BLOCKS], I32)
            pad = tb("pad", [P, MSG])
            spread = tb("spread", [P, HALVES])
            ends = tb("ends", [P, HALVES])
            sums_start = tb("sums_start", [P, HALVES])
            node_int = tb("node_int", [P, 2], I32)
            limit_int = tb("limit_int", [P, 1], I32)
            limit = tb("limit", [P, 1])
            bad = tb("bad", [P, 3, HALVES])
            bad_total = tb("bad_total", [P, 1])
            fits = tb("fits", [P, 1])
            disorder = tb("disorder", [STEPS, EDGES])
            ps = st.enter_context(nc.psum_tensor("ps_idx", [P, 8, 512], F32))
            loaded = sem("setup_loaded")
            highest_saved = sem("highest_saved")
            highest_loaded = sem("highest_loaded")
            start_saved = sem("start_saved")
            start_loaded = sem("start_loaded")
            pads_saved = sem("pads_saved")
            cleared = sem("setup_cleared")
            consts = sem("setup_consts")
            dve = sem("setup_dve")
            turned = sem("setup_turned")
            judged = sem("judged")
            START_DONE = 43
            full = E // EDGES
            rest = E - full * EDGES

            with nc.Block() as block:
                @block.sync
                def _(sp):
                    for i, v in enumerate((wl_t, wr_t, w)):
                        sp.dma_start(weights[:, i, :], v).then_inc(loaded, 16)
                    for i, v in enumerate((bl, gamma, beta)):
                        sp.dma_start(vectors[:, i, :], v.rearrange("(d a) -> d a", a=1)).then_inc(loaded, 16)
                    sp.dma_start(b_row[:, :], b.rearrange("(a d) -> a d", a=1).to_broadcast([P, D])).then_inc(loaded, 16)
                    sp.wait_ge(cleared, 1)
                    for i, v in enumerate((src, dst)):
                        sp.dma_start(idx_int[0:full, i, :], v[0:full * EDGES].rearrange("(s e) -> s e", e=EDGES)).then_inc(loaded, 16)
                        sp.dma_start(idx_int[full:full + 1, i, 0:rest], v[full * EDGES:E].rearrange("(s e) -> s e", s=1)).then_inc(loaded, 16)
                    sp.wait_ge(cleared, 2)
                    sp.dma_start(next_int[0:full, :], dst[1:1 + full * EDGES].rearrange("(s e) -> s e", e=EDGES)).then_inc(loaded, 16)
                    sp.dma_start(next_int[full:full + 1, 0:rest - 1], dst[full * EDGES + 1:E].rearrange("(s e) -> s e", s=1)).then_inc(loaded, 16)
                    sp.wait_ge(dve, 2)
                    sp.dma_start(group_dram.rearrange("i (s g) -> (i s) g", g=GROUPS), highest[:, :]).then_inc(highest_saved, 16)
                    sp.wait_ge(highest_saved, 16)
                    sp.dma_start(all_highest[:, :], group_dram.to_broadcast([P, STEPS * GROUPS])).then_inc(highest_loaded, 16)
                    sp.wait_ge(consts, 7)
                    for m in msg_dram:
                        sp.dma_start(rows(m, EPAD, P, 1), pad[:, :]).then_inc(pads_saved, 16)
                    sp.wait_ge(dve, START_DONE)
                    sp.dma_start(start_dram.rearrange("i (s b) -> (i s) b", b=BLOCKS), start_i[0:STEPS, :]).then_inc(start_saved, 16)
                    sp.wait_ge(start_saved, 16)
                    sp.dma_start(starts_all[:, :], start_dram).then_inc(start_loaded, 16)
                    sp.wait_ge(start_loaded, 16)
                    sp.wait_ge(pads_saved, 32)
                    sp.wait_ge(loaded, 16 * 13)

                @block.gpsimd
                def _(pool):
                    pool.memset(idx_int[:, 0, :], 0).then_inc(consts, 1)
                    pool.memset(idx_int[:, 1, :], int(FAR)).then_inc(cleared, 1)
                    pool.memset(next_int[:, :], int(FAR)).then_inc(cleared, 1)
                    pool.iota(iota_int[:, :, :], pattern=[[1, 2], [2, P]], base=0, channel_multiplier=0).then_inc(consts, 1)
                    pool.iota(base_int[:, :], pattern=[[-BLOCK, STEPS * BLOCKS]], base=0, channel_multiplier=0).then_inc(consts, 1)
                    pool.iota(half_int[:, :], pattern=[[-HALF, STEPS * HALVES]], base=0, channel_multiplier=0).then_inc(consts, 1)
                    pool.iota(row_base_int[:, :], pattern=[[HALF, HALVES + 1]], base=0, channel_multiplier=NODES).then_inc(consts, 1)
                    pool.memset(pad[:, :], FAR).then_inc(consts, 1)
                    pool.memset(ident[:, :], 0.0).then_inc(consts, 1)
                    pool.wait_ge(consts, 7)
                    pool.affine_select(out=ident[:, :], in_=ident[:, :], compare_op=ALU.not_equal, fill=1.0, base=0,
                                       pattern=[[-1, P]], channel_multiplier=1).then_inc(consts, 1)
                    pool.memset(ones[:, :], 1.0).then_inc(consts, 1)
                    pool.memset(eps[:, :], EPS).then_inc(consts, 1)
                    pool.memset(starts_none[:, :], EPAD).then_inc(consts, 1)
                    pool.iota(node_int[:, :], pattern=[[1, 2]], base=0, channel_multiplier=2).then_inc(consts, 1)
                    pool.iota(limit_int[:, :], pattern=[[1, 1]], base=AHEAD * EDGES, channel_multiplier=EDGES).then_inc(consts, 1)

                @block.vector
                def _(v):
                    done = [0]

                    def then(ins):
                        done[0] += 1
                        ins.then_inc(dve, 1)
                        v.wait_ge(dve, done[0])

                    v.wait_ge(loaded, 16 * 13)
                    then(v.tensor_copy(idx_f[:, :, :], idx_int[:, :, :]))
                    then(v.tensor_reduce(highest[:, :], idx_f[:, 1, :].rearrange("s (g e) -> s g e", e=GROUP), axis=AX.X, op=ALU.max))
                    v.wait_ge(consts, 13)
                    then(v.tensor_copy(iota[:, :, :], iota_int[:, :, :]))
                    then(v.tensor_copy(negbase[:, :], base_int[:, :]))
                    then(v.tensor_copy(negbase_half[:, :], half_int[:, :]))
                    then(v.tensor_copy(row_base[:, :], row_base_int[:, :]))
                    then(v.tensor_copy(node_col[:, :], node_int[:, :]))
                    then(v.tensor_copy(limit[:, :], limit_int[:, :]))
                    then(v.tensor_scalar(sums_start[:, :], row_base[:, 0:HALVES], float(SUMS_ROW), None, ALU.add))
                    v.wait_ge(turned, 8)
                    for c in range(CH):
                        then(v.tensor_copy(src_col[:, :, c], ps[:, c, 0:STEPS]))
                        then(v.tensor_copy(dst_col[:, :, c], ps[:, CH + c, 0:STEPS]))
                    then(v.tensor_copy(next_f[:, :], next_int[:, :]))
                    then(v.tensor_tensor(disorder[:, :], idx_f[:, 1, :], next_f[:, :], ALU.is_gt))
                    v.wait_ge(highest_loaded, 16)
                    for g in range(HALVES + 1):
                        then(v.tensor_scalar(cmp_out[:, :], all_highest[:, :], row_base[:, g:g + 1], None, ALU.is_lt,
                                             ALU.add, accum_out=below[:, g:g + 1]))
                    then(v.tensor_scalar(start_f[:, :], below[:, 0:HALVES], float(GROUP), None, ALU.mult))
                    then(v.memset(bad[:, :, :], 0.0))
                    then(v.tensor_tensor(spread[:, :], below[:, 1:HALVES + 1], below[:, 0:HALVES], ALU.subtract))
                    then(v.tensor_scalar(bad[0:STEPS, 0, :], spread[0:STEPS, :], float(WINDOW // GROUP - 1), None, ALU.is_gt))
                    then(v.tensor_scalar(ends[:, :], start_f[:, :], float(WINDOW), float(EPAD), ALU.add, ALU.min))
                    then(v.tensor_scalar(bad[0:STEPS, 1, :], ends[0:STEPS, :], limit[0:STEPS, :], None, ALU.is_gt))
                    then(v.tensor_reduce(bad[0:STEPS, 2, 0:1], disorder[:, :], axis=AX.X, op=ALU.max))
                    then(v.tensor_reduce(bad_total[:, :], bad[:, :, :], axis=AX.XY, op=ALU.add))
                    v.wait_ge(judged, 1)
                    then(v.tensor_scalar(fits[:, :], ps[:, 0, 0:1], 0.5, None, ALU.is_lt))
                    then(v.tensor_scalar(unfit[:, :], ps[0:1, 0, 0:1], 0.5, None, ALU.is_gt))
                    then(v.tensor_tensor(start_f[:, :], start_f[:, :], sums_start[:, :], ALU.subtract))
                    then(v.scalar_tensor_tensor(out=start_f[:, :], in0=start_f[:, :], scalar=fits[:, :], in1=sums_start[:, :],
                                                op0=ALU.mult, op1=ALU.add))
                    first, second = (start_f[:, :].rearrange("p (b h) -> p b h", h=2)[:, :, h] for h in range(2))
                    then(v.tensor_tensor(start_pair[:, :], second, first, ALU.subtract))
                    then(v.scalar_tensor_tensor(out=start_pair[:, :], in0=start_pair[:, :], scalar=1.0 / GROUP, in1=first,
                                                op0=ALU.mult, op1=ALU.add))
                    then(v.tensor_copy(start_i[:, :], start_pair[:, :]))
                    assert done[0] == START_DONE

                @block.tensor
                def _(pe):
                    pe.wait_ge(consts, 9)
                    pe.wait_ge(dve, 1)
                    for i in range(2):
                        for c in range(CH):
                            pe.transpose(ps[:, CH * i + c, 0:STEPS], idx_f[:, i, :].rearrange("s (p c) -> s c p", c=CH)[:, c, :],
                                         ident[0:STEPS, 0:STEPS]).then_inc(turned, 1)
                    pe.wait_ge(dve, START_DONE - 7)
                    pe.matmul(ps[:, 0, 0:1], ones[:, :], bad_total[:, :], start=True, stop=True).then_inc(judged, 1)

        PER_LOAD = 7
        LOADS = STEPS // PER_LOAD
        assert LOADS * PER_LOAD == STEPS

        def sum_all_pairs(table, tag):
            with stage(nc, tag) as (st, sem):
                edges = sb("pairs_edges" + tag, [P, PER_LOAD, CH * MSG], F32, st)
                sel = sb("pairs_sel" + tag, [P, CH, BLOCKS, 2, P], F32, st)
                node_rows = sb("pairs_rows" + tag, [P, BLOCKS, 2, MSG], F32, st)
                zeros = sb("pairs_zeros" + tag, [P, 512], F32, st)
                ps = st.enter_context(nc.psum_tensor("pairs_ps" + tag, [P, BLOCKS, 512], F32))
                loaded, stored, rows_ready, sel_ready, used, summed, zeroed, sp_passed, dve_passed = (
                    sem("pairs_" + n) for n in
                    ("loaded", "stored", "rows_ready", "sel_ready", "used", "summed", "zeroed", "sp_passed", "dve_passed"))

                with nc.Block() as block:
                    @block.sync
                    def _(sp):
                        sp.wait_ge(zeroed, 2)
                        with sp.Fori(0, STEPS) as t:
                            with sp.Fori(0, LOADS) as g:
                                sp.wait_ge(used, t * (STEPS + 1) + g * PER_LOAD + 1)
                                sp.dma_start(edges[:, :, :], table[bass.ds(g * (PER_LOAD * EDGES), PER_LOAD * EDGES), :]
                                             .rearrange("(e p c) m -> p e (c m)", p=P, c=CH)).then_inc(loaded, 16)
                            sp.wait_ge(rows_ready, t + 1)
                            sp.dma_start(table[bass.ds(t * NODES + SUMS_ROW, NODES), :].rearrange("(b p j) m -> p b (j m)", p=P, j=2),
                                         node_rows[:, :, :, :].rearrange("p b j m -> p b (j m)")).then_inc(stored, 16)
                            sp.wait_ge(stored, 16 * t + 16)
                            settle(sp, sp_passed)

                    @block.gpsimd
                    def _(pool):
                        pool.memset(zeros[:, :], 0.0).then_inc(zeroed, 1)
                        pool.memset(node_rows[:, :, :, D + 2:MSG], 0.0).then_inc(zeroed, 1)

                    @block.vector
                    def _(v):
                        with v.Fori(0, STEPS) as t:
                            with v.Fori(0, LOADS) as g:
                                v.wait_ge(loaded, t * (16 * LOADS) + g * 16 + 16)
                                settle(v, dve_passed)
                                with v.Fori(0, PER_LOAD) as e:
                                    v.wait_ge(used, t * (STEPS + 1) + g * PER_LOAD + e + 1)
                                    for c in range(CH):
                                        for b in range(BLOCKS):
                                            last = v.tensor_scalar(
                                                sel[:, c, b, :, :], iota[:, :, :],
                                                edges[:, bass.ds(e, 1), c * MSG + D + 1:c * MSG + D + 2].rearrange("p e m -> p (e m)"),
                                                negbase[:, bass.ds(t * BLOCKS + b, 1)], ALU.subtract, ALU.is_equal)
                                    last.then_inc(sel_ready, 1)
                            v.wait_ge(used, t * (STEPS + 1) + STEPS + 1)
                            v.tensor_copy(node_rows[:, :, :, 0:D + 1], ps[:, :, 0:2 * P].rearrange("p b (j d) -> p b j d", j=2)[:, :, :, 0:D + 1]
                                          ).then_inc(summed, 1)
                            for b in range(BLOCKS):
                                last = v.tensor_scalar(node_rows[:, b, :, D + 1], node_col[:, :], negbase[:, bass.ds(t * BLOCKS + b, 1)], None,
                                                       ALU.subtract)
                            last.then_inc(rows_ready, 1)

                    @block.tensor
                    def _(pe):
                        pe.wait_ge(zeroed, 1)
                        pe.sem_inc(summed, 1)
                        with pe.Fori(0, STEPS) as t:
                            pe.wait_ge(summed, t + 1)
                            for b in range(BLOCKS):
                                last = pe.matmul(ps[:, b, :], zeros[:, 0:P], zeros[:, :], start=True, stop=False, skip_group_check=True)
                            last.then_inc(used, 1)
                            with pe.Fori(0, STEPS) as e:
                                pe.wait_ge(sel_ready, t * STEPS + e + 1)
                                for c in range(CH):
                                    for b in range(BLOCKS):
                                        for j in range(2):
                                            last = pe.matmul(ps[:, b, j * P:j * P + D + 1], sel[:, c, b, j, :],
                                                             edges[:, bass.ds(e % PER_LOAD, 1), c * MSG:c * MSG + D + 1].rearrange("p e m -> p (e m)"),
                                                             start=False, stop=False, skip_group_check=True)
                                last.then_inc(used, 1)

        def layer0(starts, tag):
            with stage(nc, tag) as (st, sem):
                def tb(name, shape, dt=F32):
                    return sb(name + tag, shape, dt, st)

                def pb(name, banks):
                    return st.enter_context(nc.psum_tensor(name + tag, [P, banks, 512], F32))

                idx = [tb(f"idx{i}", [P, CH], U32) for i in range(4)]
                gathered = [tb(f"gathered{i}", [P, CH, D]) for i in range(4)]
                own = [tb(f"own{i}", [P, SUB, D]) for i in range(2)]
                ln_raw = tb("ln_raw", [P, TILES, 6])
                ln_tmp = tb("ln_tmp", [P, 4, TILES])
                mean2 = tb("mean2", [P, TILES])
                std = [tb(f"std{i}", [P, TILES]) for i in range(2)]
                rstd = [tb(f"rstd{i}", [P, TILES]) for i in range(2)]
                centred = [tb(f"centred{i}", [P, TILES, D]) for i in range(2)]
                turned_x = [tb(f"turned_x{i}", [D, TILES * P]) for i in range(2)]
                msg = [tb(f"msg{i}", [P, CH, MSG]) for i in range(4)]
                h = [tb(f"h{i}", [P, SUB, D + 1]) for i in range(UNROLL)]
                agg = tb("agg", [P, SUB, D])
                deg = tb("deg", [P, SUB])
                inv = tb("inv", [P, SUB])
                win = [tb(f"win{i}", [P, HALVES, MSG]) for i in range(4)]
                rel = tb("rel", [P, HALVES])
                sel = tb("sel", [P, HALVES, 2, HALF // 2])
                ps_t = pb("ps_t", 2)
                ps_m = pb("ps_m", 3)
                ps_a = pb("ps_a", 2)
                ps_g = pb("ps_g", 1)

                sp_passed = sem("sp_passed")
                pool_passed = sem("pool_passed")
                idx_ready = sem("idx_ready")
                g_loaded = [sem(f"g_loaded{i}") for i in range(4)]
                own_loaded = [sem(f"own_loaded{i}") for i in range(2)]
                own_cleared = sem("own_cleared")
                xs_stored = [sem(f"xs_stored{i}") for i in range(4)]
                ln_sem = sem("ln_sem")
                std_ready = sem("std_ready")
                rstd_ready = sem("rstd_ready")
                centred_ready = sem("centred_ready")
                t_ready = sem("t_ready")
                tx_ready = sem("tx_ready")
                m_ready = sem("m_ready")
                msg_ready = sem("msg_ready")
                msg_init = sem("msg_init")
                msg_stored = [sem(f"msg_stored{i}") for i in range(4)]
                hd_ready = sem("hd_ready")
                win_loaded = [sem(f"win_loaded{i}") for i in range(4)]
                rel_ready = sem("rel_ready")
                sel_ready = sem("sel_ready")
                agg_ready = sem("agg_ready")
                inv_sem = sem("inv_sem")
                agg_scaled = sem("agg_scaled")
                h_ready = sem("h_ready")
                h_init = sem("h_init")
                squared = sem("squared")
                gram_saved = sem("gram_saved")
                h_stored = [sem(f"h_stored{i}") for i in range(4)]

                def block_rows(ap, n, b):
                    return rows(ap, n * NODES + b * BLOCK, P, 2)

                with nc.Block() as block:
                    @block.sync
                    def _(sp):
                        def load_windows(t):
                            m = t.back(-2)
                            used = 2 * t.n - 4
                            if not t.fixed:
                                used = sp.snap(used)
                            if t.fixed and t.k == 0:
                                for k in range(2):
                                    sp.wait_ge(msg_stored[k], 16)
                            if m.exists():
                                wait(sp, msg_stored[m.slot], 16 * (m.uses + 1))
                            if not t.fixed:
                                settle(sp, sp_passed)
                            wait(sp, agg_ready, used)
                            if not t.fixed:
                                settle(sp, sp_passed)
                            load_step_windows(nc, sp, msg_dram[0], starts[0:1, bass.ds(t.n * BLOCKS, BLOCKS)], win[t.slot], win_loaded[t.slot])

                        def step(s):
                            if s.back(LAG - 1).exists():
                                load_windows(s.back(LAG - 1))

                        run_steps(sp, step)

                    @block.gpsimd
                    def _(pool):
                        def gather(s):
                            wait(pool, idx_ready, s.n + 1)
                            wait(pool, centred_ready, 2 * s.back(4).n + 1)
                            wait(pool, xs_stored[s.slot], 16 * s.uses)
                            settle(pool, pool_passed)
                            for c in range(CH):
                                pool.indirect_dma_start(
                                    out=gathered[s.slot][:, c, :], out_offset=None, in_=x,
                                    in_offset=bass.IndirectOffsetOnAxis(ap=idx[s.slot][:, c:c + 1], axis=0)).then_inc(g_loaded[s.slot], 16)

                        def step(s):
                            if s.fixed and s.k == 0:
                                gather(s)
                                gather(s.back(-1))
                            if s.back(-2).exists():
                                gather(s.back(-2))
                            t = s.back(LAG + 1)
                            if t.exists():
                                wait(pool, agg_scaled, 2 * t.n + 2)
                                wait(pool, hd_ready, 2 * t.n + 2)
                                pool.tensor_tensor(h[t.ring][:, :, 0:D], h[t.ring][:, :, 0:D], agg[:, :, :], ALU.add).then_inc(h_ready, 1)

                        for i in range(4):
                            pool.memset(msg[i][:, :, D:D + 1], 1.0).then_inc(msg_init, 1)
                            pool.memset(msg[i][:, :, D + 2:MSG], 0.0).then_inc(msg_init, 1)
                        for i in range(UNROLL):
                            pool.memset(h[i][:, :, D:D + 1], 1.0).then_inc(h_init, 1)
                        run_steps(pool, step)

                    @block.vector
                    def _(v):
                        def copy_idx(s):
                            v.tensor_copy(idx[s.slot][:, :], src_col[:, bass.ds(s.n, 1), :].rearrange("p s c -> p (s c)")).then_inc(idx_ready, 1)

                        def step(s):
                            m, t, u = s.back(1), s.back(LAG + 1), s.back(LAG)
                            if s.fixed and s.k == STEPS - 2:
                                v.wait_ge(centred_ready, 2 * s.k)
                                v.memset(own[(STEPS - 1) % 2][:, :, :], 0.0).then_inc(own_cleared, 1)
                            if t.exists():
                                wait(v, agg_ready, 2 * t.n + 2)
                                v.tensor_scalar(deg[:, :], ps_a[:, :, :].rearrange("p k (a d) -> p k a d", a=4)[:, :, :, D],
                                                1.0, None, ALU.max).then_inc(inv_sem, 1)
                            if s.fixed and s.k == 0:
                                copy_idx(s)
                                copy_idx(s.back(-1))
                            if s.exists():
                                wait(v, g_loaded[s.slot], 16 * CH * (s.uses + 1))
                                if s.back(-2).exists():
                                    copy_idx(s.back(-2))
                                for c in range(CH):
                                    v.bn_stats(ln_raw[:, c, :], gathered[s.slot][:, c, :])
                            if t.exists():
                                wait(v, inv_sem, 3 * t.n + 1)
                                wait(v, agg_scaled, 2 * t.n)
                                v.reciprocal(inv[:, :], deg[:, :]).then_inc(inv_sem, 1)
                            if s.exists():
                                wait(v, own_loaded[s.par], 16 * (s.half + 1 + (TAIL_BLOCKS if s.fixed and s.k == STEPS - 1 else 0)))
                                for c in range(SUB):
                                    last = v.bn_stats(ln_raw[:, CH + c, :], own[s.par][:, c, :])
                                last.then_inc(ln_sem, 1)
                            if t.exists():
                                wait(v, inv_sem, 3 * t.n + 2)
                                v.tensor_scalar(inv_deg[:, bass.ds(t.n, 1), :].rearrange("p s a -> p (s a)"), inv[:, :],
                                                1.0, None, ALU.mult).then_inc(inv_sem, 1)
                            if u.exists():
                                wait(v, win_loaded[u.slot], 16 * HALVES * (u.uses + 1))
                                wait(v, sel_ready, 2 * u.n)
                                v.tensor_tensor(rel[:, :], win[u.slot][:, :, D + 1], negbase_half[:, bass.ds(u.n * HALVES, HALVES)], ALU.add
                                                ).then_inc(rel_ready, 1)
                            if s.exists():
                                wait(v, ln_sem, 4 * s.n + 1)
                                even, odd = ln_raw[:, :, 1], ln_raw[:, :, 4]
                                v.tensor_tensor(mean2[:, :], even, odd, ALU.add)
                                v.tensor_tensor(ln_tmp[:, 0, :], even, odd, ALU.subtract)
                                v.tensor_tensor(ln_tmp[:, 1, :], ln_raw[:, :, 2], ln_raw[:, :, 5], ALU.add).then_inc(ln_sem, 1)
                            if m.exists():
                                wait(v, msg_stored[m.slot], 16 * m.uses)
                                v.tensor_copy(msg[m.slot][:, :, D + 1], dst_col[:, bass.ds(m.n, 1), :].rearrange("p s c -> p (s c)")).then_inc(msg_ready, 1)
                            if s.exists():
                                wait(v, ln_sem, 4 * s.n + 2)
                                v.tensor_tensor(ln_tmp[:, 2, :], ln_tmp[:, 0, :], ln_tmp[:, 0, :], ALU.mult).then_inc(ln_sem, 1)
                                wait(v, ln_sem, 4 * s.n + 3)
                                wait(v, std_ready, s.n)
                                v.scalar_tensor_tensor(out=ln_tmp[:, 3, :], in0=ln_tmp[:, 2, :], scalar=D / 4.0, in1=ln_tmp[:, 1, :],
                                                       op0=ALU.mult, op1=ALU.add).then_inc(ln_sem, 1)
                            if m.exists():
                                wait(v, m_ready, 3 * m.n + 1)
                                v.tensor_tensor(msg[m.slot][:, :, 0:D], ps_m[:, 0, 0:CH * D].rearrange("p (c d) -> p c d", d=D),
                                                rstd[m.par][:, 0:CH].unsqueeze(2).to_broadcast([P, CH, D]), ALU.mult).then_inc(msg_ready, 1)
                            if u.exists():
                                wait(v, rel_ready, u.n + 1)
                                for k in range(2):
                                    half = slice(k * HALVES // 2, (k + 1) * HALVES // 2)
                                    wait(v, agg_ready, 2 * u.back(1).n + k + 1)
                                    v.tensor_tensor(sel[:, half, :, :], iota[:, :, 0:HALF // 2].unsqueeze(1).to_broadcast([P, HALVES // 2, 2, HALF // 2]),
                                                    rel[:, half].unsqueeze(2).unsqueeze(3).to_broadcast([P, HALVES // 2, 2, HALF // 2]),
                                                    ALU.is_equal).then_inc(sel_ready, 1)
                            if s.exists():
                                wait(v, std_ready, s.n + 1)
                                v.reciprocal(rstd[s.par][:, :], std[s.par][:, :]).then_inc(rstd_ready, 1)
                                wait(v, t_ready, 3 * s.back(2).n + 3)
                                v.scalar_tensor_tensor(out=centred[s.par][:, 0:CH, :], in0=mean2[:, 0:CH].unsqueeze(2).to_broadcast([P, CH, D]),
                                                       scalar=-0.5, in1=gathered[s.slot][:, :, :], op0=ALU.mult, op1=ALU.add).then_inc(centred_ready, 1)
                                v.scalar_tensor_tensor(out=centred[s.par][:, CH:TILES, :], in0=mean2[:, CH:TILES].unsqueeze(2).to_broadcast([P, SUB, D]),
                                                       scalar=-0.5, in1=own[s.par][:, :, :], op0=ALU.mult, op1=ALU.add).then_inc(centred_ready, 1)

                        run_steps(v, step)
                        v.wait_ge(squared, STEPS + 1)
                        v.tensor_copy(gram[:, :], ps_g[0:D, 0, 0:D + 1]).then_inc(gram_saved, 1)
                        v.wait_ge(gram_saved, 1)

                    @block.scalar
                    def _(act):
                        def load_own(s):
                            wait(act, centred_ready, 2 * s.back(2).n + 2)
                            if s.fixed and s.k == STEPS - 1:
                                wait(act, own_cleared, 1)
                                for b in range(TAIL_BLOCKS):
                                    act.dma_start(own[s.par][:, 2 * b:2 * b + 2, :].rearrange("p j d -> p (j d)"),
                                                 block_rows(x, s.n, b)).then_inc(own_loaded[s.par], 16)
                                act.dma_start(own[s.par][0:TAIL_PARTS, 2 * TAIL_BLOCKS:2 * TAIL_BLOCKS + 2, :].rearrange("p j d -> p (j d)"),
                                             rows(x, s.n * NODES + TAIL_BLOCKS * BLOCK, TAIL_PARTS, 2)).then_inc(own_loaded[s.par], 16)
                            else:
                                act.dma_start(own[s.par][:, :, :].rearrange("p (b j) d -> p b (j d)", j=2),
                                             x[bass.ds(s.n * NODES, NODES), :].rearrange("(b p j) d -> p b (j d)", p=P, j=2)
                                             ).then_inc(own_loaded[s.par], 16)

                        def store_h(t):
                            wait(act, h_ready, t.n + 1)
                            act.dma_start(h_dram[bass.ds(t.n * NODES, NODES), :].rearrange("(b p j) d -> p b (j d)", p=P, j=2),
                                          h[t.ring][:, :, :].rearrange("p (b j) d -> p b (j d)", j=2)).then_inc(h_stored[t.slot], 16)

                        def step(s):
                            m, t = s.back(1), s.back(LAG + 1)
                            if s.fixed and s.k == 0:
                                load_own(s)
                            if s.back(-1).exists():
                                load_own(s.back(-1))
                            if t.back(1).exists():
                                store_h(t.back(1))
                            if t.exists():
                                wait(act, inv_sem, 3 * t.n + 2)
                                wait(act, h_ready, t.n)
                                for k in range(2):
                                    for c in range(4):
                                        a = 4 * k + c
                                        last = act.activation(agg[:, a, :], ps_a[:, k, c * P:c * P + D], ACT.Copy,
                                                              scale=inv[:, a:a + 1])
                                    last.then_inc(agg_scaled, 1)
                            if m.exists():
                                r = m.back(UNROLL)
                                wait(act, h_stored[r.slot], 16 * (r.uses + 1) + 1)
                                wait(act, squared, r.n + 2)
                                wait(act, rstd_ready, m.n + 1)
                            for k in range(2):
                                if m.exists():
                                    wait(act, m_ready, 3 * m.n + 2 + k)
                                    for c in range(4):
                                        a = 4 * k + c
                                        last = act.activation(h[m.ring][:, a, 0:D], ps_m[:, 1 + k, c * D:(c + 1) * D], ACT.Copy,
                                                              scale=rstd[m.par][:, CH + a:CH + a + 1])
                                    last.then_inc(hd_ready, 1)
                                if k == 0 and s.exists():
                                    wait(act, ln_sem, 4 * s.n + 4)
                                    act.activation(std[s.par][:, :], ln_tmp[:, 3, :], ACT.Sqrt, scale=1.0 / D, bias=eps[:, :]).then_inc(std_ready, 1)
                                    wait(act, g_loaded[s.slot], 16 * CH * (s.uses + 1))
                                    act.dma_start(rows(xsrc_dram, s.n * EDGES, P, CH),
                                                  gathered[s.slot][:, :, :].rearrange("p c d -> p (c d)")).then_inc(xs_stored[s.slot], 16)
                            if m.exists():
                                wait(act, msg_ready, 2 * m.n + 2)
                                act.dma_start(rows(msg_dram[0], m.n * EDGES, P, CH),
                                              msg[m.slot][:, :, :].rearrange("p c d -> p (c d)")).then_inc(msg_stored[m.slot], 16)
                            if s.exists():
                                wait(act, m_ready, 3 * s.back(2).n + 3)
                                for k in range(3):
                                    wait(act, t_ready, 3 * s.n + 1 + k)
                                    act.activation(turned_x[s.par][:, k * 512:(k + 1) * 512], ps_t[0:D, (s.par + k) % 2, :], ACT.Relu).then_inc(tx_ready, 1)

                        act.wait_ge(msg_init, 8)
                        act.wait_ge(h_init, UNROLL)
                        for k in range(4):
                            act.sem_inc(h_stored[k], 1)
                        act.sem_inc(squared, 1)
                        run_steps(act, step)
                        for k in range(4):
                            act.wait_ge(h_stored[k], 16 * len(range(k, STEPS, 4)) + 1)
                        for k in range(4):
                            act.wait_ge(msg_stored[k], 16 * len(range(k, STEPS, 4)))
                            act.wait_ge(xs_stored[k], 16 * len(range(k, STEPS, 4)))

                    @block.tensor
                    def _(pe):
                        def step(s):
                            m = s.back(1)
                            if m.exists():
                                for k in range(3):
                                    wait(pe, tx_ready, 3 * m.n + 1 + k)
                                    if k == 0:
                                        wait(pe, msg_ready, 2 * m.n)
                                    else:
                                        wait(pe, hd_ready, 2 * m.back(1).n + k)
                                    for c in range(4):
                                        a = 4 * k + c
                                        last = pe.matmul(ps_m[:, k, c * D:(c + 1) * D], turned_x[m.par][:, a * P:(a + 1) * P],
                                                         weights[:, 0 if k == 0 else 1, :], start=True, stop=True)
                                    last.then_inc(m_ready, 1)
                            u = s.back(LAG)
                            if u.exists():
                                wait(pe, win_loaded[u.slot], 16 * HALVES * (u.uses + 1))
                                for k in range(2):
                                    wait(pe, agg_scaled, 2 * u.back(1).n + 1 + k)
                                    wait(pe, sel_ready, 2 * u.n + 1 + k)
                                    for b in (2 * k, 2 * k + 1):
                                        for j in range(2):
                                            c = 2 * (b % 2) + j
                                            for i in range(2):
                                                last = pe.matmul(ps_a[64 * i:64 * i + 64, k, c * P:c * P + D + 1], sel[:, 2 * b + i, j, :],
                                                                 win[u.slot][:, 2 * b + i, 0:D + 1], start=True, stop=True)
                                    last.then_inc(agg_ready, 1)
                            if s.exists():
                                for k in range(3):
                                    wait(pe, centred_ready, 2 * s.n + (1 if k == 0 else 2))
                                    wait(pe, tx_ready, 3 * s.n + k - 1)
                                    for c in range(4):
                                        last = pe.transpose(ps_t[0:D, (s.par + k) % 2, c * P:(c + 1) * P], centred[s.par][:, 4 * k + c, :], ident[:, :])
                                    last.then_inc(t_ready, 1)
                            t = s.back(LAG + 1)
                            if t.exists():
                                wait(pe, h_ready, t.n + 1)
                                for a in range(SUB):
                                    last = pe.matmul(ps_g[0:D, 0, 0:D + 1], h[t.ring][:, a, 0:D], h[t.ring][:, a, :],
                                                     start=(t.fixed and t.k == 0 and a == 0),
                                                     stop=(t.fixed and t.k == STEPS - 1 and a == SUB - 1))
                                last.then_inc(squared, 1)

                        pe.wait_ge(h_init, UNROLL)
                        run_steps(pe, step)

        def batch_norm():
            with stage(nc) as (st, sem):
                squares = sb("bn_squares", [D, D], F32, st)
                moment = sb("bn_moment", [D, 2], F32, st)
                tmp = sb("bn_tmp", [D, 4], F32, st)
                affine = sb("bn_affine", [D, 2], F32, st)
                spread = sb("bn_spread", [D, 2, D], F32, st)
                ps = st.enter_context(nc.psum_tensor("ps_bn", [P, 512], F32))
                dve, spread_ready, root = sem("bn_dve"), sem("bn_spread_ready"), sem("bn_root")
                BL, GAMMA, BETA = (vectors[:, i, :] for i in range(3))
                with nc.Block() as block:
                    @block.vector
                    def _(v):
                        done = [0]

                        def then(ins):
                            done[0] += 1
                            ins.then_inc(dve, 1)
                            v.wait_ge(dve, done[0])

                        then(v.tensor_tensor(squares[:, :], gram[:, 0:D], ident[0:D, 0:D], ALU.mult))
                        then(v.tensor_reduce(moment[:, 1:2], squares[:, :], axis=AX.X, op=ALU.add))
                        then(v.tensor_scalar(moment[:, 0:1], gram[:, D:D + 1], 1.0 / N, None, ALU.mult))
                        then(v.tensor_scalar(moment[:, 1:2], moment[:, 1:2], 1.0 / N, None, ALU.mult))
                        then(v.tensor_tensor(tmp[:, 0:1], moment[:, 0:1], moment[:, 0:1], ALU.mult))
                        then(v.tensor_tensor(tmp[:, 1:2], moment[:, 1:2], tmp[:, 0:1], ALU.subtract))
                        then(v.tensor_scalar(tmp[:, 1:2], tmp[:, 1:2], 0.0, None, ALU.max))
                        v.wait_ge(root, 1)
                        then(v.reciprocal(tmp[:, 2:3], tmp[:, 2:3]))
                        then(v.tensor_tensor(affine[:, 0:1], tmp[:, 2:3], GAMMA, ALU.mult))
                        then(v.tensor_tensor(moment[:, 0:1], moment[:, 0:1], BL, ALU.add))
                        then(v.tensor_tensor(tmp[:, 3:4], BL, moment[:, 0:1], ALU.subtract))
                        then(v.tensor_tensor(tmp[:, 3:4], tmp[:, 3:4], affine[:, 0:1], ALU.mult))
                        then(v.tensor_tensor(affine[:, 1:2], tmp[:, 3:4], BETA, ALU.add))
                        for i in range(2):
                            then(v.tensor_scalar(spread[:, i, :], ident[0:D, 0:D], affine[:, i:i + 1], None, ALU.mult))
                        v.wait_ge(spread_ready, 1)
                        then(v.tensor_copy(bn[:, :, :], ps[:, 0:2 * D].rearrange("p (i d) -> p i d", d=D)))

                    @block.tensor
                    def _(pe):
                        pe.wait_ge(dve, 15)
                        pe.matmul(ps[:, 0:2 * D], ones[0:D, :], spread[:, :, :].rearrange("p i d -> p (i d)"), start=True, stop=True
                                  ).then_inc(spread_ready, 1)

                    @block.scalar
                    def _(act):
                        act.wait_ge(dve, 7)
                        act.activation(tmp[:, 2:3], tmp[:, 1:2], ACT.Sqrt, bias=eps[0:D, :]).then_inc(root, 1)

        def layer1(starts, tag):
            with stage(nc, tag) as (st, sem):
                def tb(name, shape, dt=F32):
                    return sb(name + tag, shape, dt, st)

                def pb(name, banks):
                    return st.enter_context(nc.psum_tensor(name + tag, [P, banks, 512], F32))

                idx = [tb(f"idx1_{i}", [P, CH], U32) for i in range(4)]
                gathered = [tb(f"h_src{i}", [P, CH, D + 1]) for i in range(4)]
                xs = [tb(f"x_src{i}", [P, CH, D]) for i in range(2)]
                x2 = [tb(f"x2_src{i}", [P, CH, D]) for i in range(2)]
                ln_raw = tb("ln1_raw", [P, CH, 6])
                ln_tmp = tb("ln1_tmp", [P, 4, CH])
                mean2 = tb("mean2_1", [P, CH])
                std = [tb(f"std1_{i}", [P, CH]) for i in range(2)]
                rstd = [tb(f"rstd1_{i}", [P, CH]) for i in range(2)]
                centred = [tb(f"centred1_{i}", [P, CH, D]) for i in range(2)]
                turned_x = [tb(f"turned1_{i}", [D, CH * P]) for i in range(2)]
                msg = [tb(f"msg1_{i}", [P, CH, MSG]) for i in range(4)]
                xn = [tb(f"x_own{i}", [P, SUB, D]) for i in range(4)]
                hn = [tb(f"h_own{i}", [P, SUB, D + 1]) for i in range(4)]
                agg = tb("agg1", [P, SUB, D])
                win = [tb(f"win1_{i}", [P, HALVES, MSG]) for i in range(4)]
                rel = tb("rel1", [P, HALVES])
                sel = tb("sel1", [P, HALVES, 2, HALF // 2])
                ps_t = pb("ps1_t", 2)
                ps_m = pb("ps1_m", 2)
                ps_a = pb("ps1_a", 4)

                sp_passed = sem("sp1_passed")
                pool_passed = sem("pool1_passed")
                idx_ready = sem("idx1_ready")
                g_loaded = [sem(f"h_src_loaded{i}") for i in range(4)]
                xs_loaded = [sem(f"x_src_loaded{i}") for i in range(2)]
                x2_ready = sem("x2_ready")
                ln_sem = sem("ln1_sem")
                std_ready = sem("std1_ready")
                rstd_ready = sem("rstd1_ready")
                centred_ready = sem("centred1_ready")
                t_ready = sem("t1_ready")
                tx_ready = sem("tx1_ready")
                m_ready = sem("m1_ready")
                scaled = sem("msg1_scaled")
                msg_ready = sem("msg1_ready")
                msg_stored = [sem(f"msg1_stored{i}") for i in range(4)]
                msg_init = sem("msg1_init")
                own_cleared = sem("own1_cleared")
                xn_loaded = [sem(f"x_own_loaded{i}") for i in range(4)]
                hn_loaded = [sem(f"h_own_loaded{i}") for i in range(4)]
                win_loaded = [sem(f"win1_loaded{i}") for i in range(4)]
                normed = sem("normed")
                shifted = sem("shifted")
                rel_ready = sem("rel1_ready")
                sel_ready = sem("sel1_ready")
                agg_ready = sem("agg1_ready")
                agg_scaled = sem("agg1_scaled")
                out_ready = sem("out_ready")
                out_stored = [sem(f"out_stored{i}") for i in range(4)]

                with nc.Block() as block:
                    @block.sync
                    def _(sp):
                        def load_windows(t):
                            m = t.back(-2)
                            used = 4 * t.n - 8
                            if not t.fixed:
                                used = sp.snap(used)
                            if t.fixed and t.k == 0:
                                for k in range(2):
                                    sp.wait_ge(msg_stored[k], 16)
                            if m.exists():
                                wait(sp, msg_stored[m.slot], 16 * (m.uses + 1))
                            if not t.fixed:
                                settle(sp, sp_passed)
                            wait(sp, agg_ready, used)
                            if not t.fixed:
                                settle(sp, sp_passed)
                            load_step_windows(nc, sp, msg_dram[1], starts[0:1, bass.ds(t.n * BLOCKS, BLOCKS)], win[t.slot], win_loaded[t.slot])

                        def step(s):
                            if s.back(LAG - 1).exists():
                                load_windows(s.back(LAG - 1))

                        run_steps(sp, step)

                    @block.gpsimd
                    def _(pool):
                        def gather(s):
                            wait(pool, idx_ready, s.n + 1)
                            wait(pool, x2_ready, 3 * s.back(4).n + 3)
                            settle(pool, pool_passed)
                            for c in range(CH):
                                pool.indirect_dma_start(
                                    out=gathered[s.slot][:, c, :], out_offset=None, in_=h_dram,
                                    in_offset=bass.IndirectOffsetOnAxis(ap=idx[s.slot][:, c:c + 1], axis=0)).then_inc(g_loaded[s.slot], 16)

                        def step(s):
                            if s.fixed and s.k == 0:
                                gather(s)
                                gather(s.back(-1))
                            if s.back(-2).exists():
                                gather(s.back(-2))
                            u = s.back(LAG)
                            if u.exists():
                                slot, uses = u.slot, u.uses
                                wait(pool, hn_loaded[slot], 16 * (uses + 1))
                                pool.tensor_tensor(hn[slot][:, :, 0:D], hn[slot][:, :, 0:D], bn[:, 0, :].unsqueeze(1).to_broadcast([P, SUB, D]),
                                                   ALU.mult).then_inc(normed, 1)
                                wait(pool, normed, 2 * u.n + 1)
                                pool.tensor_tensor(hn[slot][:, 0:POOL_SHIFTS, 0:D], hn[slot][:, 0:POOL_SHIFTS, 0:D],
                                                   bn[:, 1, :].unsqueeze(1).to_broadcast([P, POOL_SHIFTS, D]),
                                                   ALU.add).then_inc(normed, 1)

                        for i in range(4):
                            pool.memset(msg[i][:, :, D:D + 1], 1.0).then_inc(msg_init, 1)
                            pool.memset(msg[i][:, :, D + 2:MSG], 0.0).then_inc(msg_init, 1)
                        run_steps(pool, step)

                    @block.vector
                    def _(v):
                        def copy_idx(s):
                            v.tensor_copy(idx[s.slot][:, :], src_col[:, bass.ds(s.n, 1), :].rearrange("p s c -> p (s c)")).then_inc(idx_ready, 1)

                        def step(s):
                            m, t, u = s.back(1), s.back(LAG + 1), s.back(LAG)
                            g, z = gathered[s.slot], x2[s.par]
                            if s.fixed and s.k == 0:
                                copy_idx(s)
                                copy_idx(s.back(-1))
                            if s.exists():
                                wait(v, g_loaded[s.slot], 16 * CH * (s.uses + 1))
                                if s.back(-2).exists():
                                    copy_idx(s.back(-2))
                                wait(v, centred_ready, s.n - 1)
                                v.tensor_tensor(z[:, :, :], g[:, :, 0:D], bn[:, 0, :].unsqueeze(1).to_broadcast([P, CH, D]), ALU.mult).then_inc(x2_ready, 1)
                            if t.exists():
                                wait(v, normed, 2 * t.n + 1)
                                v.tensor_tensor(hn[t.slot][:, POOL_SHIFTS:SUB, 0:D], hn[t.slot][:, POOL_SHIFTS:SUB, 0:D],
                                                bn[:, 1, :].unsqueeze(1).to_broadcast([P, SUB - POOL_SHIFTS, D]), ALU.add).then_inc(shifted, 1)
                            if s.exists():
                                wait(v, x2_ready, 3 * s.n + 1)
                                v.tensor_tensor(z[:, :, :], z[:, :, :], bn[:, 1, :].unsqueeze(1).to_broadcast([P, CH, D]), ALU.add).then_inc(x2_ready, 1)
                            if t.exists():
                                slot, uses = t.slot, t.uses
                                wait(v, shifted, t.n + 1)
                                wait(v, normed, 2 * t.n + 2)
                                wait(v, xn_loaded[slot], 16 * (uses + 1 + (TAIL_BLOCKS if t.fixed and t.k == STEPS - 1 else 0)))
                                v.scalar_tensor_tensor(out=xn[slot][:, :, :], in0=hn[slot][:, :, 0:D], scalar=0.0, in1=xn[slot][:, :, :],
                                                       op0=ALU.max, op1=ALU.add).then_inc(out_ready, 1)
                            if s.exists():
                                wait(v, x2_ready, 3 * s.n + 2)
                                wait(v, xs_loaded[s.par], 16 * (s.half + 1))
                                v.scalar_tensor_tensor(out=z[:, :, :], in0=z[:, :, :], scalar=0.0, in1=xs[s.par][:, :, :],
                                                       op0=ALU.max, op1=ALU.add).then_inc(x2_ready, 1)
                                wait(v, x2_ready, 3 * s.n + 3)
                                for c in range(CH):
                                    last = v.bn_stats(ln_raw[:, c, :], z[:, c, :])
                                last.then_inc(ln_sem, 1)
                            if u.exists():
                                wait(v, win_loaded[u.slot], 16 * HALVES * (u.uses + 1))
                                wait(v, sel_ready, 2 * u.n)
                                v.tensor_tensor(rel[:, :], win[u.slot][:, :, D + 1], negbase_half[:, bass.ds(u.n * HALVES, HALVES)], ALU.add
                                                ).then_inc(rel_ready, 1)
                            if s.exists():
                                wait(v, ln_sem, 4 * s.n + 1)
                                even, odd = ln_raw[:, :, 1], ln_raw[:, :, 4]
                                v.tensor_tensor(mean2[:, :], even, odd, ALU.add)
                                v.tensor_tensor(ln_tmp[:, 0, :], even, odd, ALU.subtract)
                                v.tensor_tensor(ln_tmp[:, 1, :], ln_raw[:, :, 2], ln_raw[:, :, 5], ALU.add).then_inc(ln_sem, 1)
                            if m.exists():
                                wait(v, msg_stored[m.slot], 16 * m.uses)
                                v.tensor_copy(msg[m.slot][:, :, D + 1], dst_col[:, bass.ds(m.n, 1), :].rearrange("p s c -> p (s c)")).then_inc(msg_ready, 1)
                            if s.exists():
                                wait(v, ln_sem, 4 * s.n + 2)
                                v.tensor_tensor(ln_tmp[:, 2, :], ln_tmp[:, 0, :], ln_tmp[:, 0, :], ALU.mult).then_inc(ln_sem, 1)
                                wait(v, ln_sem, 4 * s.n + 3)
                                wait(v, std_ready, s.n)
                                v.scalar_tensor_tensor(out=ln_tmp[:, 3, :], in0=ln_tmp[:, 2, :], scalar=D / 4.0, in1=ln_tmp[:, 1, :],
                                                       op0=ALU.mult, op1=ALU.add).then_inc(ln_sem, 1)
                            if u.exists():
                                wait(v, rel_ready, u.n + 1)
                                for k in range(2):
                                    half = slice(k * HALVES // 2, (k + 1) * HALVES // 2)
                                    wait(v, agg_ready, 4 * u.back(1).n + 2 * k + 2)
                                    v.tensor_tensor(sel[:, half, :, :], iota[:, :, 0:HALF // 2].unsqueeze(1).to_broadcast([P, HALVES // 2, 2, HALF // 2]),
                                                    rel[:, half].unsqueeze(2).unsqueeze(3).to_broadcast([P, HALVES // 2, 2, HALF // 2]),
                                                    ALU.is_equal).then_inc(sel_ready, 1)
                            if s.exists():
                                wait(v, std_ready, s.n + 1)
                                v.reciprocal(rstd[s.par][:, :], std[s.par][:, :]).then_inc(rstd_ready, 1)
                                wait(v, t_ready, s.n - 1)
                                v.scalar_tensor_tensor(out=centred[s.par][:, :, :], in0=mean2[:, :].unsqueeze(2).to_broadcast([P, CH, D]),
                                                       scalar=-0.5, in1=x2[s.par][:, :, :], op0=ALU.mult, op1=ALU.add).then_inc(centred_ready, 1)
                            if t.exists():
                                wait(v, out_ready, 2 * t.n + 1)
                                wait(v, agg_scaled, 4 * t.n + 4)
                                v.tensor_tensor(xn[slot][:, :, :], xn[slot][:, :, :], agg[:, :, :], ALU.add).then_inc(out_ready, 1)
                                if t.fixed and t.k == STEPS - 4:
                                    tail_slot = (STEPS - 1) % 4
                                    v.wait_ge(out_stored[tail_slot], 16 * ((STEPS - 1) // 4) + 1)
                                    v.memset(xn[tail_slot][:, :, :], 0.0).then_inc(own_cleared, 1)
                            if m.exists():
                                wait(v, scaled, m.n + 1)
                                v.tensor_tensor(msg[m.slot][:, :, 0:D], msg[m.slot][:, :, 0:D], b_row[:, :].unsqueeze(1).to_broadcast([P, CH, D]),
                                                ALU.add).then_inc(msg_ready, 1)

                        run_steps(v, step)

                    @block.scalar
                    def _(act):
                        def load_xs(s):
                            wait(act, x2_ready, 3 * s.back(2).n + 3)
                            act.dma_start(xs[s.par][:, :, :].rearrange("p c d -> p (c d)"), rows(xsrc_dram, s.n * EDGES, P, CH)
                                         ).then_inc(xs_loaded[s.par], 16)

                        def load_h(t):
                            slot, uses = t.slot, t.uses
                            wait(act, out_stored[slot], 16 * uses + 1)
                            act.dma_start(hn[slot][:, :, :].rearrange("p (b j) d -> p b (j d)", j=2),
                                         h_dram[bass.ds(t.n * NODES, NODES), :].rearrange("(b p j) d -> p b (j d)", p=P, j=2)
                                         ).then_inc(hn_loaded[slot], 16)

                        def load_x(t):
                            slot, uses = t.slot, t.uses
                            wait(act, out_stored[slot], 16 * uses + 1)
                            if t.fixed and t.k == STEPS - 1:
                                act.wait_ge(own_cleared, 1)
                                for b in range(TAIL_BLOCKS):
                                    act.dma_start(xn[slot][:, 2 * b:2 * b + 2, :].rearrange("p j d -> p (j d)"),
                                                 rows(x, t.n * NODES + b * BLOCK, P, 2)).then_inc(xn_loaded[slot], 16)
                                act.dma_start(xn[slot][0:TAIL_PARTS, 2 * TAIL_BLOCKS:2 * TAIL_BLOCKS + 2, :].rearrange("p j d -> p (j d)"),
                                             rows(x, t.n * NODES + TAIL_BLOCKS * BLOCK, TAIL_PARTS, 2)).then_inc(xn_loaded[slot], 16)
                            else:
                                act.dma_start(xn[slot][:, :, :].rearrange("p (b j) d -> p b (j d)", j=2),
                                             x[bass.ds(t.n * NODES, NODES), :].rearrange("(b p j) d -> p b (j d)", p=P, j=2)
                                             ).then_inc(xn_loaded[slot], 16)

                        def scale_sums(u, blocks):
                            for b in blocks:
                                wait(act, agg_ready, 4 * u.n + b + 1)
                                for j in range(2):
                                    a = 2 * b + j
                                    last = act.activation(agg[:, a, :], ps_a[:, b, j * P:j * P + D], ACT.Copy,
                                                          scale=inv_deg[:, bass.ds(u.n, 1), a:a + 1].rearrange("p s a -> p (s a)"))
                                last.then_inc(agg_scaled, 1)

                        def step(s):
                            m, t, u = s.back(1), s.back(LAG + 1), s.back(LAG)
                            if s.fixed and s.k == 0:
                                load_xs(s)
                            if s.exists():
                                wait(act, ln_sem, 4 * s.n + 4)
                                act.activation(std[s.par][:, :], ln_tmp[:, 3, :], ACT.Sqrt, scale=1.0 / D, bias=eps[:, :]).then_inc(std_ready, 1)
                            if t.exists():
                                scale_sums(t, range(BLOCKS // 2, BLOCKS))
                            if s.back(-1).exists():
                                load_xs(s.back(-1))
                            if s.back(LAG - 1).exists():
                                load_h(s.back(LAG - 1))
                            if s.exists():
                                wait(act, t_ready, s.n + 1)
                                wait(act, m_ready, s.n - 1)
                                act.activation(turned_x[s.par][:, :], ps_t[0:D, s.par, :], ACT.Relu).then_inc(tx_ready, 1)
                            if t.exists():
                                slot = t.slot
                                wait(act, out_ready, 2 * t.n + 2)
                                if t.fixed and t.k == STEPS - 1:
                                    for b in range(TAIL_BLOCKS):
                                        act.dma_start(rows(out, t.n * NODES + b * BLOCK, P, 2),
                                                     xn[slot][:, 2 * b:2 * b + 2, :].rearrange("p j d -> p (j d)")).then_inc(out_stored[slot], 16)
                                    act.dma_start(rows(out, t.n * NODES + TAIL_BLOCKS * BLOCK, TAIL_PARTS, 2),
                                                 xn[slot][0:TAIL_PARTS, 2 * TAIL_BLOCKS:2 * TAIL_BLOCKS + 2, :].rearrange("p j d -> p (j d)")
                                                 ).then_inc(out_stored[slot], 16)
                                else:
                                    act.dma_start(out[bass.ds(t.n * NODES, NODES), :].rearrange("(b p j) d -> p b (j d)", p=P, j=2),
                                                 xn[slot][:, :, :].rearrange("p (b j) d -> p b (j d)", j=2)).then_inc(out_stored[slot], 16)
                            if u.exists():
                                wait(act, out_ready, 2 * u.n)
                                scale_sums(u, range(0, BLOCKS // 2))
                            if s.exists():
                                wait(act, m_ready, s.n + 1)
                                wait(act, rstd_ready, s.n + 1)
                                wait(act, msg_stored[s.slot], 16 * s.uses)
                                for c in range(CH):
                                    last = act.activation(msg[s.slot][:, c, 0:D], ps_m[:, s.par, c * D:(c + 1) * D], ACT.Copy, scale=rstd[s.par][:, c:c + 1])
                                last.then_inc(scaled, 1)
                            if s.back(LAG - 1).exists():
                                load_x(s.back(LAG - 1))
                            if m.exists():
                                wait(act, msg_ready, 2 * m.n + 2)
                                act.dma_start(rows(msg_dram[1], m.n * EDGES, P, CH),
                                             msg[m.slot][:, :, :].rearrange("p c d -> p (c d)")).then_inc(msg_stored[m.slot], 16)

                        act.wait_ge(msg_init, 8)
                        for slot in range(4):
                            act.sem_inc(out_stored[slot], 1)
                        run_steps(act, step)
                        for k in range(4):
                            act.wait_ge(msg_stored[k], 16 * len(range(k, STEPS, 4)))
                        for slot in range(4):
                            uses = len(range(slot, STEPS, 4)) + (TAIL_BLOCKS if slot == (STEPS - 1) % 4 else 0)
                            act.wait_ge(out_stored[slot], 16 * uses + 1)

                    @block.tensor
                    def _(pe):
                        def sum_edges(u, blocks):
                            for b in blocks:
                                wait(pe, agg_scaled, 4 * u.back(1).n + b + 1)
                                wait(pe, sel_ready, 2 * u.n + 1 + b // 2)
                                for j in range(2):
                                    for i in range(2):
                                        last = pe.matmul(ps_a[64 * i:64 * i + 64, b, j * P:j * P + D + 1], sel[:, 2 * b + i, j, :],
                                                         win[u.slot][:, 2 * b + i, 0:D + 1], start=True, stop=True)
                                last.then_inc(agg_ready, 1)

                        def step(s):
                            if s.exists():
                                wait(pe, centred_ready, s.n + 1)
                                wait(pe, tx_ready, s.n - 1)
                                for c in range(CH):
                                    last = pe.transpose(ps_t[0:D, s.par, c * P:(c + 1) * P], centred[s.par][:, c, :], ident[:, :])
                                last.then_inc(t_ready, 1)
                            u = s.back(LAG)
                            if u.exists():
                                wait(pe, win_loaded[u.slot], 16 * HALVES * (u.uses + 1))
                                sum_edges(u, range(0, BLOCKS // 2))
                            if s.exists():
                                wait(pe, tx_ready, s.n + 1)
                                wait(pe, scaled, s.n - 1)
                                for c in range(CH):
                                    last = pe.matmul(ps_m[:, s.par, c * D:(c + 1) * D], turned_x[s.par][:, c * P:(c + 1) * P],
                                                     weights[:, 2, :], start=True, stop=True)
                                last.then_inc(m_ready, 1)
                            if u.exists():
                                sum_edges(u, range(BLOCKS // 2, BLOCKS))

                        run_steps(pe, step)

        misfit = nc.values_load(unfit[0:1, 0:1], min_val=0, max_val=1)
        with nc.If(misfit > 0):
            layer0(starts_none, "_a")
            sum_all_pairs(msg_dram[0], "_0")
        layer0(starts_all, "")
        batch_norm()
        with nc.If(misfit > 0):
            layer1(starts_none, "_a")
            sum_all_pairs(msg_dram[1], "_1")
        layer1(starts_all, "")


def kernel(x, src, dst, L0_gnn_Wl, L0_gnn_bl, L0_gnn_Wr, L0_gnn_gamma, L0_gnn_beta, L1_gnn_W, L1_gnn_b):
    import concourse.bacc as bacc
    from concourse.bass_utils import run_bass_kernel_spmd

    nc = bacc.Bacc("TRN2", target_bir_lowering=False, num_devices=1)
    given = {
        "x": x, "src": src, "dst": dst, "wl_t": np.transpose(L0_gnn_Wl), "bl": L0_gnn_bl,
        "wr_t": np.transpose(L0_gnn_Wr), "gamma": L0_gnn_gamma, "beta": L0_gnn_beta,
        "w": L1_gnn_W, "b": L1_gnn_b,
    }
    arrays, args = {}, []
    for name, a in given.items():
        a = np.ascontiguousarray(a)
        arrays[f"in_{name}"] = a
        args.append(nc.dram_tensor(f"in_{name}", a.shape, mybir.dt.from_np(a.dtype), kind="ExternalInput").ap())
    result = nc.dram_tensor("result", [N, D], F32, kind="ExternalOutput").ap()
    gnn_kernel(nc, *args, result)
    r = run_bass_kernel_spmd(nc, [arrays], core_ids=[0])
    return r.results[0]["result"]
```
